# Optimizing a Trainium2 kernel written in Bass

```python
import numpy as np
import jax
import jax.numpy as jnp

def _softmax(x, axis=-1):
    return jax.nn.softmax(x, axis=axis)

def _gelu(x):
    return jax.nn.gelu(x, approximate=True)

def _silu(x):
    return jax.nn.silu(x)

def _sigmoid(x):
    return jax.nn.sigmoid(x)

def _layernorm(x, axis=-1, eps=1e-05):
    m = jnp.mean(x, axis=axis, keepdims=True)
    v = jnp.var(x, axis=axis, keepdims=True)
    return (x - m) / jnp.sqrt(v + eps)

def _scatter_add(tgt, idx, src, axis=0):
    return tgt.at[idx].add(src)

def _segment_sum(src, seg, n):
    return jax.ops.segment_sum(src, seg, n)
kernel_name = 'mk_gnn_ffn_d1_gnn_r8_9b0137'

def setup_inputs(seed: int=0):
    np.random.seed(seed)
    _w = jnp.asarray

    def _rec_inputs():
        import jax
        import jax.numpy as jnp
        _gk = jax.random.key(seed)
        x = -0.0002117 + 1 * jax.random.normal(jax.random.fold_in(_gk, 1), (1250, 512), jnp.float32)
        _s = jax.random.randint(jax.random.fold_in(_gk, 2), (20000,), 0, 1250, jnp.int32)
        _d = jax.random.randint(jax.random.fold_in(_gk, 3), (20000,), 0, 1250, jnp.int32)
        _loop = jnp.arange(1250, dtype=jnp.int32)
        src = jnp.concatenate([_s, _d, _loop])
        dst = jnp.concatenate([_d, _s, _loop])
        _o = jnp.argsort(dst, stable=True)
        src = src[_o]
        dst = dst[_o]
        edge_attr_3 = 0.000669165 + 0.999965 * jax.random.normal(jax.random.fold_in(_gk, 11), (41250, 3), jnp.float32)
        return (x, src, dst, edge_attr_3)
    x, src, dst, edge_attr_3 = _rec_inputs()

    def _L0_gnn_setup():
        import jax, jax.numpy as jnp
        import numpy as np
        N = 6250
        E = 100000
        D_IN = 512
        D_OUT = 512
        EDGE_DIM = 3
        key = jax.random.key(seed)
        k = jax.random.split(key, 6)
        x = jax.random.normal(k[0], (N, D_IN), dtype=jnp.float32)
        edge_index = jax.random.randint(k[1], (2, E), 0, N, dtype=jnp.int64)
        edge_attr = jax.random.normal(k[2], (E, EDGE_DIM), dtype=jnp.float32)
        lim1 = (6.0 / (D_IN + D_OUT)) ** 0.5
        lin_w = jax.random.uniform(k[3], (D_OUT, D_IN), minval=-lim1, maxval=lim1, dtype=jnp.float32)
        lin_b = jnp.zeros((D_OUT,), dtype=jnp.float32)
        lim2 = (6.0 / (EDGE_DIM + 1)) ** 0.5
        conf_w = jax.random.uniform(k[4], (1, EDGE_DIM), minval=-lim2, maxval=lim2, dtype=jnp.float32)
        conf_b = jnp.zeros((1,), dtype=jnp.float32)
        return {'x': x, 'edge_index': edge_index, 'edge_attr': edge_attr, 'lin_w': lin_w, 'lin_b': lin_b, 'conf_w': conf_w, 'conf_b': conf_b}
    _L0_gnn_all = _L0_gnn_setup()
    _L0_gnn_in = {k: v for k, v in _L0_gnn_all.items() if k in ('lin_w', 'lin_b', 'conf_w', 'conf_b')}
    del _L0_gnn_all

    def _L0_ffn_setup():
        import jax, jax.numpy as jnp
        import numpy as np
        D = 512
        H = 8
        K = 4
        HD = D // H

        def _ln(x, w, b, eps=1e-05):
            m = x.mean(-1, keepdims=True)
            v = ((x - m) ** 2).mean(-1, keepdims=True)
            return (x - m) / jnp.sqrt(v + eps) * w + b

        def _spatial_experts(xn, idx, in_w, in_b, out_w, out_b):
            W = in_w[idx]
            qkv = jnp.einsum('btd,bed->bte', xn, W) + in_b[idx][:, None, :]
            q, k, v = jnp.split(qkv, 3, axis=-1)
            B, T, _ = xn.shape
            q = q.reshape(B, T, H, HD) * HD ** (-0.5)
            k = k.reshape(B, T, H, HD)
            v = v.reshape(B, T, H, HD)
            att = jax.nn.softmax(jnp.einsum('bthd,bshd->bhts', q, k), axis=-1)
            o = jnp.einsum('bhts,bshd->bthd', att, v).reshape(B, T, D)
            return jnp.einsum('btd,bod->bto', o, out_w[idx]) + out_b[idx][:, None, :]

        def _temporal_experts(xt, idx, qw, qb, kw, kb, vw, vb, pw, pb):
            B, T, _ = xt.shape
            q = (jnp.einsum('btd,bod->bto', xt, qw[idx]) + qb[idx][:, None, :]).reshape(B, T, H, HD)
            k = (jnp.einsum('btd,bod->bto', xt, kw[idx]) + kb[idx][:, None, :]).reshape(B, T, H, HD)
            v = (jnp.einsum('btd,bod->bto', xt, vw[idx]) + vb[idx][:, None, :]).reshape(B, T, H, HD)
            logits = jnp.einsum('bthd,bshd->bhts', q, k) * HD ** (-0.5)
            causal = jnp.tril(jnp.ones((T, T), dtype=bool))
            logits = jnp.where(causal, logits, -jnp.inf)
            att = jax.nn.softmax(logits, axis=-1)
            o = jnp.einsum('bhts,bshd->bthd', att, v).reshape(B, T, D)
            o = jnp.einsum('btd,bod->bto', o, pw[idx]) + pb[idx][:, None, :]
            return xt + o

        def _cross_mha(q_in, kv_in, in_w, in_b, out_w, out_b):
            B, T, _ = q_in.shape
            S = kv_in.shape[1]
            Wq, Wk, Wv = (in_w[:D], in_w[D:2 * D], in_w[2 * D:])
            bq, bk, bv = (in_b[:D], in_b[D:2 * D], in_b[2 * D:])
            q = (q_in @ Wq.T + bq).reshape(B, T, H, HD) * HD ** (-0.5)
            k = (kv_in @ Wk.T + bk).reshape(B, S, H, HD)
            v = (kv_in @ Wv.T + bv).reshape(B, S, H, HD)
            att = jax.nn.softmax(jnp.einsum('bthd,bshd->bhts', q, k), axis=-1)
            o = jnp.einsum('bhts,bshd->bthd', att, v).reshape(B, T, D)
            return o @ out_w.T + out_b
        key = jax.random.key(seed)
        ks = iter(jax.random.split(key, 40))
        B, T = (256, 64)
        p = lambda *shape: jax.random.normal(next(ks), shape, dtype=jnp.float32) * 0.02
        inp = {'x': jax.random.normal(next(ks), (B, T, D), dtype=jnp.float32), 'router_w1': p(128, D), 'router_b1': jnp.zeros((128,), jnp.float32), 'router_w2': p(2 * K, 128), 'router_b2': jnp.zeros((2 * K,), jnp.float32), 'norm_s_w': jnp.ones((D,), jnp.float32), 'norm_s_b': jnp.zeros((D,), jnp.float32), 'norm_t_w': jnp.ones((D,), jnp.float32), 'norm_t_b': jnp.zeros((D,), jnp.float32), 'sp_in_w': p(K, 3 * D, D), 'sp_in_b': jnp.zeros((K, 3 * D), jnp.float32), 'sp_out_w': p(K, D, D), 'sp_out_b': jnp.zeros((K, D), jnp.float32), 'tq_w': p(K, D, D), 'tq_b': jnp.zeros((K, D), jnp.float32), 'tk_w': p(K, D, D), 'tk_b': jnp.zeros((K, D), jnp.float32), 'tv_w': p(K, D, D), 'tv_b': jnp.zeros((K, D), jnp.float32), 'tp_w': p(K, D, D), 'tp_b': jnp.zeros((K, D), jnp.float32), 'cross_in_w': p(3 * D, D), 'cross_in_b': jnp.zeros((3 * D,), jnp.float32), 'cross_out_w': p(D, D), 'cross_out_b': jnp.zeros((D,), jnp.float32), 'norm_mlp_w': jnp.ones((D,), jnp.float32), 'norm_mlp_b': jnp.zeros((D,), jnp.float32), 'mlp_w1': p(4 * D, D), 'mlp_b1': jnp.zeros((4 * D,), jnp.float32), 'mlp_w2': p(D, 4 * D), 'mlp_b2': jnp.zeros((D,), jnp.float32)}
        return inp
    _L0_ffn_all = _L0_ffn_setup()
    _L0_ffn_in = {k: v for k, v in _L0_ffn_all.items() if k in ('router_w1', 'router_b1', 'router_w2', 'router_b2', 'norm_s_w', 'norm_s_b', 'norm_t_w', 'norm_t_b', 'sp_in_w', 'sp_in_b', 'sp_out_w', 'sp_out_b', 'tq_w', 'tq_b', 'tk_w', 'tk_b', 'tv_w', 'tv_b', 'tp_w', 'tp_b', 'cross_in_w', 'cross_in_b', 'cross_out_w', 'cross_out_b', 'norm_mlp_w', 'norm_mlp_b', 'mlp_w1', 'mlp_b1', 'mlp_w2', 'mlp_b2')}
    del _L0_ffn_all
    return {'x': x, 'src': src, 'dst': dst, 'edge_attr_3': edge_attr_3, 'L0_gnn_lin_w': _L0_gnn_in['lin_w'], 'L0_gnn_lin_b': _L0_gnn_in['lin_b'], 'L0_gnn_conf_w': _L0_gnn_in['conf_w'], 'L0_gnn_conf_b': _L0_gnn_in['conf_b'], 'L0_ffn_router_w1': _L0_ffn_in['router_w1'], 'L0_ffn_router_b1': _L0_ffn_in['router_b1'], 'L0_ffn_router_w2': _L0_ffn_in['router_w2'], 'L0_ffn_router_b2': _L0_ffn_in['router_b2'], 'L0_ffn_norm_s_w': _L0_ffn_in['norm_s_w'], 'L0_ffn_norm_s_b': _L0_ffn_in['norm_s_b'], 'L0_ffn_norm_t_w': _L0_ffn_in['norm_t_w'], 'L0_ffn_norm_t_b': _L0_ffn_in['norm_t_b'], 'L0_ffn_sp_in_w': _L0_ffn_in['sp_in_w'], 'L0_ffn_sp_in_b': _L0_ffn_in['sp_in_b'], 'L0_ffn_sp_out_w': _L0_ffn_in['sp_out_w'], 'L0_ffn_sp_out_b': _L0_ffn_in['sp_out_b'], 'L0_ffn_tq_w': _L0_ffn_in['tq_w'], 'L0_ffn_tq_b': _L0_ffn_in['tq_b'], 'L0_ffn_tk_w': _L0_ffn_in['tk_w'], 'L0_ffn_tk_b': _L0_ffn_in['tk_b'], 'L0_ffn_tv_w': _L0_ffn_in['tv_w'], 'L0_ffn_tv_b': _L0_ffn_in['tv_b'], 'L0_ffn_tp_w': _L0_ffn_in['tp_w'], 'L0_ffn_tp_b': _L0_ffn_in['tp_b'], 'L0_ffn_cross_in_w': _L0_ffn_in['cross_in_w'], 'L0_ffn_cross_in_b': _L0_ffn_in['cross_in_b'], 'L0_ffn_cross_out_w': _L0_ffn_in['cross_out_w'], 'L0_ffn_cross_out_b': _L0_ffn_in['cross_out_b'], 'L0_ffn_norm_mlp_w': _L0_ffn_in['norm_mlp_w'], 'L0_ffn_norm_mlp_b': _L0_ffn_in['norm_mlp_b'], 'L0_ffn_mlp_w1': _L0_ffn_in['mlp_w1'], 'L0_ffn_mlp_b1': _L0_ffn_in['mlp_b1'], 'L0_ffn_mlp_w2': _L0_ffn_in['mlp_w2'], 'L0_ffn_mlp_b2': _L0_ffn_in['mlp_b2']}

def reference(x, src, dst, edge_attr_3, L0_gnn_lin_w, L0_gnn_lin_b, L0_gnn_conf_w, L0_gnn_conf_b, L0_ffn_router_w1, L0_ffn_router_b1, L0_ffn_router_w2, L0_ffn_router_b2, L0_ffn_norm_s_w, L0_ffn_norm_s_b, L0_ffn_norm_t_w, L0_ffn_norm_t_b, L0_ffn_sp_in_w, L0_ffn_sp_in_b, L0_ffn_sp_out_w, L0_ffn_sp_out_b, L0_ffn_tq_w, L0_ffn_tq_b, L0_ffn_tk_w, L0_ffn_tk_b, L0_ffn_tv_w, L0_ffn_tv_b, L0_ffn_tp_w, L0_ffn_tp_b, L0_ffn_cross_in_w, L0_ffn_cross_in_b, L0_ffn_cross_out_w, L0_ffn_cross_out_b, L0_ffn_norm_mlp_w, L0_ffn_norm_mlp_b, L0_ffn_mlp_w1, L0_ffn_mlp_b1, L0_ffn_mlp_w2, L0_ffn_mlp_b2):
    import jax
    import jax.numpy as jnp

    def _L0_gnn_ref(x, edge_index, edge_attr, lin_w, lin_b, conf_w, conf_b):
        import jax, jax.numpy as jnp
        import numpy as np
        N = 6250
        E = 100000
        D_IN = 512
        D_OUT = 512
        EDGE_DIM = 3
        row, col = (edge_index[0], edge_index[1])
        edge_weight = jax.nn.sigmoid(edge_attr @ conf_w.T + conf_b)[:, 0]
        deg = jnp.zeros((x.shape[0],), dtype=x.dtype).at[row].add(1.0)
        deg_safe = jnp.where(deg > 0, deg, 1.0)
        deg_inv_sqrt = jnp.where(deg > 0, jax.lax.rsqrt(deg_safe), 0.0)
        norm = deg_inv_sqrt[row] * deg_inv_sqrt[col] * edge_weight
        norm = jnp.where(jnp.isnan(norm), 0.0, norm)
        out = jnp.zeros_like(x).at[col].add(x[row] * norm[:, None])
        return out @ lin_w.T + lin_b

    def _L0_ffn_ref(x, router_w1, router_b1, router_w2, router_b2, norm_s_w, norm_s_b, norm_t_w, norm_t_b, sp_in_w, sp_in_b, sp_out_w, sp_out_b, tq_w, tq_b, tk_w, tk_b, tv_w, tv_b, tp_w, tp_b, cross_in_w, cross_in_b, cross_out_w, cross_out_b, norm_mlp_w, norm_mlp_b, mlp_w1, mlp_b1, mlp_w2, mlp_b2):
        import jax, jax.numpy as jnp
        import numpy as np
        D = 512
        H = 8
        K = 4
        HD = D // H

        def _ln(x, w, b, eps=1e-05):
            m = x.mean(-1, keepdims=True)
            v = ((x - m) ** 2).mean(-1, keepdims=True)
            return (x - m) / jnp.sqrt(v + eps) * w + b

        def _spatial_experts(xn, idx, in_w, in_b, out_w, out_b):
            W = in_w[idx]
            qkv = jnp.einsum('btd,bed->bte', xn, W) + in_b[idx][:, None, :]
            q, k, v = jnp.split(qkv, 3, axis=-1)
            B, T, _ = xn.shape
            q = q.reshape(B, T, H, HD) * HD ** (-0.5)
            k = k.reshape(B, T, H, HD)
            v = v.reshape(B, T, H, HD)
            att = jax.nn.softmax(jnp.einsum('bthd,bshd->bhts', q, k), axis=-1)
            o = jnp.einsum('bhts,bshd->bthd', att, v).reshape(B, T, D)
            return jnp.einsum('btd,bod->bto', o, out_w[idx]) + out_b[idx][:, None, :]

        def _temporal_experts(xt, idx, qw, qb, kw, kb, vw, vb, pw, pb):
            B, T, _ = xt.shape
            q = (jnp.einsum('btd,bod->bto', xt, qw[idx]) + qb[idx][:, None, :]).reshape(B, T, H, HD)
            k = (jnp.einsum('btd,bod->bto', xt, kw[idx]) + kb[idx][:, None, :]).reshape(B, T, H, HD)
            v = (jnp.einsum('btd,bod->bto', xt, vw[idx]) + vb[idx][:, None, :]).reshape(B, T, H, HD)
            logits = jnp.einsum('bthd,bshd->bhts', q, k) * HD ** (-0.5)
            causal = jnp.tril(jnp.ones((T, T), dtype=bool))
            logits = jnp.where(causal, logits, -jnp.inf)
            att = jax.nn.softmax(logits, axis=-1)
            o = jnp.einsum('bhts,bshd->bthd', att, v).reshape(B, T, D)
            o = jnp.einsum('btd,bod->bto', o, pw[idx]) + pb[idx][:, None, :]
            return xt + o

        def _cross_mha(q_in, kv_in, in_w, in_b, out_w, out_b):
            B, T, _ = q_in.shape
            S = kv_in.shape[1]
            Wq, Wk, Wv = (in_w[:D], in_w[D:2 * D], in_w[2 * D:])
            bq, bk, bv = (in_b[:D], in_b[D:2 * D], in_b[2 * D:])
            q = (q_in @ Wq.T + bq).reshape(B, T, H, HD) * HD ** (-0.5)
            k = (kv_in @ Wk.T + bk).reshape(B, S, H, HD)
            v = (kv_in @ Wv.T + bv).reshape(B, S, H, HD)
            att = jax.nn.softmax(jnp.einsum('bthd,bshd->bhts', q, k), axis=-1)
            o = jnp.einsum('bhts,bshd->bthd', att, v).reshape(B, T, D)
            return o @ out_w.T + out_b
        pooled = x.mean(axis=1)
        h = jax.nn.gelu(pooled @ router_w1.T + router_b1, approximate=False)
        route = jax.nn.softmax(h @ router_w2.T + router_b2, axis=-1)
        idx_s = jnp.argmax(route[:, :K], axis=-1)
        idx_t = jnp.argmax(route[:, K:], axis=-1)
        xn = _ln(x, norm_s_w, norm_s_b)
        spatial_out = _spatial_experts(xn, idx_s, sp_in_w, sp_in_b, sp_out_w, sp_out_b)
        xt = _ln(x, norm_t_w, norm_t_b)
        temporal_out = _temporal_experts(xt, idx_t, tq_w, tq_b, tk_w, tk_b, tv_w, tv_b, tp_w, tp_b)
        fused = _cross_mha(spatial_out, temporal_out, cross_in_w, cross_in_b, cross_out_w, cross_out_b)
        x = x + fused
        h2 = _ln(x, norm_mlp_w, norm_mlp_b)
        x = x + (jax.nn.gelu(h2 @ mlp_w1.T + mlp_b1, approximate=False) @ mlp_w2.T + mlp_b2)
        return x
    edge_index = jnp.stack([src, dst])
    x = x + _L0_gnn_ref(_layernorm(x, axis=-1), edge_index, edge_attr_3, L0_gnn_lin_w, L0_gnn_lin_b, L0_gnn_conf_w, L0_gnn_conf_b)
    x = x + _L0_ffn_ref(_layernorm(x, axis=-1)[None], L0_ffn_router_w1, L0_ffn_router_b1, L0_ffn_router_w2, L0_ffn_router_b2, L0_ffn_norm_s_w, L0_ffn_norm_s_b, L0_ffn_norm_t_w, L0_ffn_norm_t_b, L0_ffn_sp_in_w, L0_ffn_sp_in_b, L0_ffn_sp_out_w, L0_ffn_sp_out_b, L0_ffn_tq_w, L0_ffn_tq_b, L0_ffn_tk_w, L0_ffn_tk_b, L0_ffn_tv_w, L0_ffn_tv_b, L0_ffn_tp_w, L0_ffn_tp_b, L0_ffn_cross_in_w, L0_ffn_cross_in_b, L0_ffn_cross_out_w, L0_ffn_cross_out_b, L0_ffn_norm_mlp_w, L0_ffn_norm_mlp_b, L0_ffn_mlp_w1, L0_ffn_mlp_b1, L0_ffn_mlp_w2, L0_ffn_mlp_b2)[0]
    return x

_drawn_inputs = setup_inputs


def setup_inputs(seed=0):
    import zlib

    import numpy as np

    out = dict(_drawn_inputs(seed))
    spreads = {'L0_gnn_lin_b': (0.0, 0.1),
     'L0_ffn_router_b1': (0.0, 0.462),
     'L0_ffn_router_b2': (0.0, 0.1),
     'L0_ffn_norm_s_w': (1.0, 0.6),
     'L0_ffn_norm_s_b': (0.0, 0.8),
     'L0_ffn_norm_t_w': (1.0, 0.6),
     'L0_ffn_norm_t_b': (0.0, 0.768),
     'L0_ffn_sp_in_b': (0.0, 0.8),
     'L0_ffn_sp_out_b': (0.0, 0.8),
     'L0_ffn_tq_b': (0.0, 0.8),
     'L0_ffn_tk_b': (0.0, 2.0),
     'L0_ffn_tv_b': (0.0, 0.8),
     'L0_ffn_tp_b': (0.0, 0.795),
     'L0_ffn_cross_in_b': (0.0, 0.352),
     'L0_ffn_cross_out_b': (0.0, 0.8),
     'L0_ffn_norm_mlp_w': (1.0, 0.6),
     'L0_ffn_norm_mlp_b': (0.0, 2.0),
     'L0_ffn_mlp_b1': (0.0, 1.708),
     'L0_ffn_mlp_b2': (0.0, 0.8)}
    factors = {'L0_ffn_router_w2': 4.623,
     'L0_ffn_sp_in_w': 8.0,
     'L0_ffn_sp_out_w': 8.0,
     'L0_ffn_tq_w': 8.0,
     'L0_ffn_tk_w': 8.0,
     'L0_ffn_tv_w': 8.0,
     'L0_ffn_tp_w': 8.0,
     'L0_ffn_cross_in_w': 2.876}
    for name, (base, spread) in spreads.items():
        noise = np.random.default_rng([zlib.crc32(name.encode()), seed]).standard_normal(out[name].shape)
        drawn = base * np.exp(spread * noise) if base else spread * noise
        out[name] = jnp.asarray(drawn.astype(out[name].dtype))
    for name, factor in factors.items():
        out[name] = (out[name] * factor).astype(out[name].dtype)
    return out
```

```python
from contextlib import ExitStack

import concourse.bass as bass
import numpy as np
from concourse import mybir

F32, F16, BF16, I32 = mybir.dt.float32, mybir.dt.float16, mybir.dt.bfloat16, mybir.dt.int32
ACT, ALU, AX = mybir.ActivationFunctionType, mybir.AluOpType, mybir.AxisListType

N, D, E = 1250, 512, 41250
TP = 125
NT = N // TP
EC = E // TP
KD = D // 128
H, HD = 8, 64
DFF = 4 * D
GC = 5
NG = EC // GC
WIN = 50
NW = N // WIN
WU = 8
KW = WIN * NT
PACK = 128
LS = 2048.0
HOT_PARTS = 5
WS = 64.0
ES = 1024.0
EPS = 1e-5
MASKED = -3.0e38
SPLITS = [(0, 512), (512, 1024), (1024, N)]
ACC = 1536
AV_FIRST = 3
T_BANK, O_BANK = 3072, 3584
LIN, SPK, SPQ, SPV, SPO, TMK, TMQ, TMV, TMP, CRQ, CRK, CRV, CRO, UP0, DN0 = *range(14), 17
UNITS, SLOTS = 21, 4


def build(nc, A, out):
    ctx = ExitStack()
    with ctx:
        def sb(name, shape, dt):
            return ctx.enter_context(nc.sbuf_tensor(name, shape, dt))

        def sem(name):
            return ctx.enter_context(nc.semaphore(name))

        UNIT = KD * D * 4
        ROW = NT * D * 4
        R1, R2, R3 = 0, ROW, 2 * ROW
        QKV = 3 * ROW
        PPT = QKV + 4 * ROW
        OREG = PPT + ROW + 4608
        WST = OREG + 7168
        WSL = WST + UNIT
        arena = sb("arena", [128, (WSL + SLOTS * UNIT) // 4], F32)

        def view(at, dt, *dims, parts=128):
            size = 2 if dt in (F16, BF16) else 4
            n = int(np.prod(dims)) * size
            n4 = (n + 3) // 4
            v = arena[0:parts, at // 4:at // 4 + n4]
            if dt != F32:
                v = v.bitcast(dt)
            v = v[:, 0:int(np.prod(dims))]
            if len(dims) == 2:
                v = v.rearrange("p (a b) -> p a b", b=dims[1])
            if len(dims) == 3:
                v = v.rearrange("p (a b c) -> p a b c", b=dims[1], c=dims[2])
            return v

        HALF = ROW // 2

        def pair(at):
            return view(at, F16, KD, N), view(at + HALF, F16, KD, N)

        adj = view(R1, F32, NT, N, parts=TP)
        src_i = view(R1, I32, EC, parts=TP)
        dst_i = view(R1 + 1400, I32, EC, parts=TP)
        attr = view(R1 + 2800, F32, 3, EC, parts=TP)
        dst_g = view(R1 + 7000, I32, GC * TP, parts=NG)
        hi_hot = view(R1 + 9600, F16, EC, NT, parts=TP)
        ew = view(R1 + 16400, F32, EC, parts=TP)
        win_v = view(R1 + 18000, F32, 2 * NW, parts=NG)
        win_t = view(R1 + 20000, F32, NW, parts=NG)
        src_f = view(R1 + 22000, F32, EC, parts=TP)
        w16 = view(R1 + 24000, F16, EC, parts=TP)
        lo_hot = view(QKV, F16, EC, TP, parts=TP)
        EA = PPT + 2560
        src_hi = view(EA, F32, EC, parts=TP)
        src_lo = view(EA + 1400, F32, EC, parts=TP)
        krel = [view(EA + 2800, F32, EC, parts=TP), view(EA + 4200, F32, EC, parts=TP)]
        w_hi = view(EA + 5600, F32, EC, parts=TP)
        w_lo = view(EA + 7000, F32, EC, parts=TP)
        w_ratio = view(EA + 8400, F32, EC, parts=TP)
        key_hot = view(PPT + 14100, F16, GC, KW, parts=TP)
        low_part = [view(PPT + 20400 + 2048 * i, F32, KW, parts=TP) for i in range(2)]
        low_hot = view(PPT + 19120, F16, GC, TP, parts=TP)
        xs = view(WSL + UNIT, F32, NT, D, parts=TP)
        agg = pair(QKV)
        x1 = view(QKV + ROW, F32, NT, D, parts=TP)
        xb = view(QKV + 2 * ROW, F32, NT, D, parts=TP)
        x0 = xb
        z0 = view(QKV + 3 * ROW, F32, NT, D, parts=TP)
        xn, xt = pair(R1), pair(R3)
        at_, so, to = pair(R1), pair(R2), pair(R3)
        QA = view(QKV, F16, H, N)
        QB = view(QKV + ROW, F16, H, N)
        K2 = view(QKV + 2 * ROW, F16, H, N)
        V = view(QKV + 3 * ROW, F16, NT, H, 2 * HD, parts=TP)
        prob = [view(PPT + i * 5000, F32, N, parts=TP) for i in range(2)]
        probT = view(PPT + 10000, F32, NT, TP, parts=TP)
        pT_hi = [view(PPT + 15000 + i * 2500, F16, NT, TP, parts=TP) for i in range(2)]
        pT_lo = [view(PPT + 20000 + i * 2500, F16, NT, TP, parts=TP) for i in range(2)]
        y32 = [view(PPT + i * 5000, F32, N) for i in range(2)]
        part_hi = [view(PPT + 10000 + i * 2500, F16, N) for i in range(2)]
        part_lo = [view(PPT + 15000 + i * 2500, F16, N) for i in range(2)]
        otok = [view(OREG + i * 2048, F32, D, parts=TP) for i in range(2)]
        osum = view(OREG + 4096, F32, H // 2, HD, parts=TP)
        oT = view(OREG + 5120, F32, KD, TP)
        x2 = view(R2, F32, NT, D, parts=TP)
        z2 = view(R3, F32, NT, D, parts=TP)
        x1b = z2
        h2 = pair(R1)
        gT = (view(QKV, F16, DFF // 128, N), view(QKV + 2 * ROW, F16, DFF // 128, N))
        w_in = view(WST, F32, KD, D)
        WH = [view(WSL + i * UNIT, F16, KD, D) for i in range(SLOTS)]
        WL = [view(WSL + i * UNIT + UNIT // 2, F16, KD, D) for i in range(SLOTS)]

        ident = sb("ident", [128, 128], F32)
        ident_b = sb("ident_b", [TP, TP], BF16)
        mask = sb("mask", [TP, TP], BF16)
        iota = sb("iota", [TP, KW], F16)
        zeros = sb("zeros", [TP, TP], F16)
        bb = [sb(f"bias_rows{i}", [TP, D], F32) for i in range(2)]
        win25 = view(EA + 11400, F32, NW, parts=NG)
        group1 = sb("group1", [NG, 1], F32)
        groupr = sb("groupr", [NG, 1], F32)
        dmm = sb("dmm", [NG, 2], F32)
        rmax = sb("rmax", [2 * NW, 1], F32)
        rows = view(EA + 9800, F32, 4, 64, parts=1)
        visits = view(EA + 11000, I32, NW + 1, parts=1)
        confw = sb("confw", [TP, 4], F32)
        stat = sb("stat", [TP, NT, 6], F32)
        mv = sb("mv", [TP, NT, 2], F32)
        rstd = sb("rstd", [TP, NT], F32)
        nmr = sb("nmr", [TP, NT], F32)
        var = sb("var", [TP, NT], F32)
        newton = sb("newton", [TP, NT], F32)
        deg = sb("deg", [TP, NT], F32)
        dis = sb("dis", [TP, NT], F32)
        dis_s = sb("dis_s", [TP, NT], F32)
        ones = sb("ones", [TP, 1], F32)
        kw_col = sb("kw_col", [TP, 1], F32)
        deg3 = sb("deg3", [3 * NT, 3 * TP], F32)
        norms = sb("norms", [128, 6, KD], F32)
        sp_b = sb("sp_b", [128, 2, KD], F32)
        sp_ob = sb("sp_ob", [128, KD], F32)
        tm_b = sb("tm_b", [128, 3, KD], F32)
        cr_b = sb("cr_b", [128, 2, KD], F32)
        up_b = sb("up_b", [128, 16], F32)
        q_b = sb("q_b", [128, 3, KD], F32)
        rw1 = view(WST, F32, KD, 128)
        rw2 = sb("rw2", [128, 8], F32)
        rb1 = sb("rb1", [128, 1], F32)
        rb2 = sb("rb2", [1, 8], F32)
        pooled = sb("pooled", [128, KD], F32)
        hid = sb("hid", [128, 1], F32)
        rt = sb("rt", [1, 8, 8], F32)
        chosen = sb("chosen", [1, 2], I32)
        nmax = sb("nmax", [TP, 2], F32)
        rsum = sb("rsum", [TP, 2, H], F32)
        rinv = sb("rinv", [TP, 2, H], F32)
        PS = ctx.enter_context(nc.psum_tensor("PS", [128, 4096], F32))

        x1_d = nc.dram_tensor("x1_spill", (NT, TP, D), F32, kind="Internal").ap()
        x0_d = nc.dram_tensor("x0_spill", (NT, TP, D), F32, kind="Internal").ap()

        edges_in, conf_in, cols_in, x_in, xr_in = (sem(s) for s in ("edges_in", "conf_in", "cols_in", "x_in", "xr_in"))
        linb_in, rw_in = sem("linb_in"), sem("rw_in")
        consts = sem("consts")
        pool_ch = sem("pool_ch")
        dve_ch = sem("dve_ch")
        act_ch = sem("act_ch")
        logit_ready, ew_ready = sem("logit_ready"), sem("ew_ready")
        lo_ready, hi_ready = sem("lo_ready"), sem("hi_ready")
        bounds_ready, boundsT, rmax_ready, rows_done, visits_ready = (
            sem(s) for s in ("bounds_ready", "boundsT", "rmax_ready", "rows_done", "visits_ready"))
        deg_done, deg3_ready, deg_root, xs_scale, xs_ready = (
            sem(s) for s in ("deg_done", "deg3_ready", "deg_root", "xs_scale", "xs_ready"))
        krel_ready, win_free, win_done, win_high, low_added = (
            sem(s) for s in ("krel_ready", "win_free", "win_done", "win_high", "low_added"))
        hot_free = [sem(f"hot_free{g}") for g in range(GC)]
        key_made = [sem(f"key_made{g}") for g in range(GC)]
        low_made = [sem(f"low_made{g}") for g in range(GC)]
        w_loaded, w_taken, w_split = sem("w_loaded"), sem("w_taken"), sem("w_split")
        accF_done, accF_read = sem("accF_done"), sem("accF_read")
        v_hi, v_split = sem("v_hi"), sem("v_split")
        accT_done, accT_free = sem("accT_done"), sem("accT_free")
        y_split, hi_done, res_done, o_ch = sem("y_split"), sem("hi_done"), sem("res_done"), sem("o_ch")
        k_moved, q_moved = [sem(f"k_moved{b}") for b in range(2)], [sem(f"q_moved{b}") for b in range(2)]
        xb_ready, var_ready, std_ready = sem("xb_ready"), sem("var_ready"), sem("std_ready")
        x0_ready, z0_ready, spilled, x0_in, x0b_ready = (
            sem(s) for s in ("x0_ready", "z0_ready", "spilled", "x0_in", "x0b_ready"))
        r_pool, r_poolc, r_hid, r_gelu, r_log, r_max, r_exp, r_idx = (
            sem(s) for s in ("r_pool", "r_poolc", "r_hid", "r_gelu", "r_log", "r_max", "r_exp", "r_idx"))
        zT_done, zT_act, zT_dve, spb_in, tmb_in = (sem(s) for s in ("zT_done", "zT_act", "zT_dve", "spb_in", "tmb_in"))
        rows_in = {s: sem(f"rows_{s}_in") for s in ("SPV", "TMV", "CRV", "CRO", "DN")}
        qb_ready = sem("qb_ready")
        z2_ready, x1_in, x1b_ready, out_done = (sem(s) for s in ("z2_ready", "x1_in", "x1b_ready", "out_done"))
        att = [{s: sem(f"{a}_{s}") for s in ("s_done", "max_done", "exp_done", "t_full", "t_free", "t2_full", "t2_free", "av_done",
                                             "o_read", "o_ready", "oT_hi", "oT_lo", "hi_0", "hi_1", "hi_2",
                                             "lo_0", "lo_1", "lo_2")} for a in ("sp", "tm", "cr")]

        block = ctx.enter_context(nc.Block())
        f_tiles, t_tiles = [0], [0]

        FBASE, TBASE = {}, {}
        for name, n in (("agg", 4), ("SPK", 4), ("SPQ", 4), ("SPO", 4), ("TMK", 4), ("TMQ", 4), ("TMP", 4),
                        ("CRQ", 4), ("CRK", 4), ("UP0", 4), ("UP1", 4), ("UP2", 4), ("UP3", 4)):
            FBASE[name] = f_tiles[0]
            f_tiles[0] += n
        for name in ("LIN", "SPV", "TMV", "CRV", "CRO", "DN"):
            TBASE[name] = t_tiles[0]
            t_tiles[0] += NT

        def key_tiles(a, T):
            return T + 1 if a == 1 else NT

        def chunks(a, T):
            n = key_tiles(a, T)
            return [(c, min(c + 4, n)) for c in range(0, n, 4)]

        def t_before(a, T, h, c=0):
            per = [min(len(chunks(a, t)), 2) for t in range(T + 1)]
            turns = H * sum(per[:T]) + h * per[T] + min(c, per[T])
            return turns + (max(T - 1, 0) + (1 if T >= 1 and h > 2 else 0))

        def tile_columns(T, it):
            return slice(T * TP, (T + 1) * TP) if isinstance(it, int) else bass.ds(it * (2 * TP) + T * TP, TP)

        def third_group(h):
            return ((h + 1) % 2) * ACC + N

        def c_before(a, T, h, c):
            return (T - (4 * c if a == 1 else 0)) * H + h

        def wait_split(engine, a, which, T, h, c, it, done):
            n = c_before(a, T, h, c) + done
            if n:
                engine.wait_ge(att[a][f"{which}_{c}"], n + it * PER2["step"])

        def attention_tiles(engine, a, body):
            if a == 1:
                for T in range(NT):
                    body(T, 0)
                return
            body(0, 0)
            body(1, 0)
            with engine.Fori(0, 3) as it:
                body(2, it)
                body(3, it)
            body(8, 0)
            body(9, 0)

        def windows(engine, body, before_window=None, after_window=None):
            def window(ww, j, packed):
                at = slice(NW, NW + 1) if isinstance(ww, int) else bass.ds(ww * WU + (j + 1), 1)
                after = engine.value_load(visits[0:1, at], min_val=0, max_val=NW * NG * PACK)
                if before_window:
                    before_window(ww, j)
                with engine.Fori(packed // PACK, after // PACK) as visit:
                    group = nc.s_assert_within(visit - packed // PACK + packed % PACK, 0, NG - 1,
                                               skip_runtime_bounds_check_because="the table bounds it")
                    body(j, visit, group)
                if after_window:
                    after_window(ww, j)
                return after

            with engine.Fori(0, NW // WU) as ww:
                packed = engine.value_load(visits[0:1, bass.ds(ww * WU, 1)], min_val=0, max_val=NW * NG * PACK)
                for j in range(WU):
                    packed = window(ww, j, packed)
            last = engine.value_load(visits[0:1, NW - 1:NW], min_val=0, max_val=NW * NG * PACK)
            window(NW // WU, 0, last)

        def window_adj(ww, j):
            at = slice(WIN * (WU * ww + j), WIN * (WU * ww + j + 1)) if isinstance(ww, int) else bass.ds(ww * (WU * WIN) + j * WIN, WIN)
            return adj[:, :, at].rearrange("p a d -> p d a")

        def keys_moved(engine, count):
            for b in range(2):
                engine.wait_ge(k_moved[b], 64 + 128 * count)

        def queries_moved(engine, count):
            for b in range(2):
                engine.wait_ge(q_moved[b], 128 + 256 * count)

        def heads_moved(engine, count):
            keys_moved(engine, count)
            queries_moved(engine, count)

        PER2 = {"step": 2 * H, "turn": 2 * (H * 2 + 1), "tile": 2, "half": 4}

        @block.sync
        def _(sp):
            sp.dma_start(dst_g, A["dst_g"]).then_inc(edges_in, 16)
            sp.dma_start(src_i, A["src_t"]).then_inc(edges_in, 16)
            sp.dma_start(dst_i, A["dst_t"]).then_inc(edges_in, 16)
            sp.dma_start(attr, A["attr_t"]).then_inc(edges_in, 16)
            sp.dma_start(xs, A["x"].rearrange("(t p) d -> p t d", p=TP)).then_inc(x_in, 16)

            def load(unit, src):
                if unit >= 1:
                    sp.wait_ge(w_taken, unit)
                sp.dma_start(w_in, src).then_inc(w_loaded, 16)

            load(LIN, A["lin_w"])
            sp.wait_ge(win_done, NW)
            sp.dma_start(xb, A["x"].rearrange("(t p) d -> p t d", p=TP)).then_inc(xr_in, 16)
            sp.wait_ge(w_taken, 1)
            sp.dma_start(rw1, A["r_w1"]).then_inc(rw_in, 16)
            sp.wait_ge(x0_ready, 1)
            sp.dma_start(x1_d.rearrange("t p d -> p t d"), x1).then_inc(spilled, 16)
            sp.wait_ge(x0_ready, 2)
            sp.dma_start(x0_d.rearrange("t p d -> p t d"), x0).then_inc(spilled, 16)
            sp.wait_ge(r_idx, 1)
            si = sp.value_load(chosen[0:1, 0:1], min_val=0, max_val=3)
            ti = sp.value_load(chosen[0:1, 1:2], min_val=0, max_val=3)
            ds = bass.ds

            sp.wait_ge(r_hid, 1)
            load(SPK, A["sp_w"][ds(si, 1), 1].rearrange("a p k o -> p (a k) o"))
            sp.dma_start(sp_b[:, :, :], A["sp_kqb"][ds(si, 1)].rearrange("a p u k -> p (a u) k")).then_inc(spb_in, 16)
            sp.dma_start(sp_ob[:, :], A["sp_ob"][ds(si, 1)].rearrange("a p k -> p (a k)")).then_inc(spb_in, 16)
            sp.dma_start(bb[1][:, :], A["sp_vb"][ds(si, 1), :].broadcast_to([TP, D])).then_inc(rows_in["SPV"], 16)
            sp.dma_start(tm_b[:, :, :], A["tm_kqpb"][ds(ti, 1)].rearrange("a p u k -> p (a u) k")).then_inc(tmb_in, 16)
            load(SPQ, A["sp_w"][ds(si, 1), 0].rearrange("a p k o -> p (a k) o"))
            load(SPV, A["sp_w"][ds(si, 1), 2].rearrange("a p k o -> p (a k) o"))
            sp.dma_start(bb[0][:, :], A["tm_vb"][ds(ti, 1), :].broadcast_to([TP, D])).then_inc(rows_in["TMV"], 16)

            def move_heads(fbase, is_q):
                with sp.Fori(0, 2) as mm:
                    for b in range(2):
                        m = mm * 2 + b
                        sp.wait_ge(y_split, m + (fbase + 1 + 2))
                        hi, lo = part_hi[b], part_lo[b]
                        for half, h in ((slice(0, 64), m * 2), (slice(64, 128), m * 2 + 1)):
                            if is_q:
                                for to_ in (slice(0, 64), slice(64, 128)):
                                    sp.dma_start(QA[to_, ds(h, 1), :], hi[half, :]).then_inc(q_moved[b], 16)
                                    sp.dma_start(QB[to_, ds(h, 1), :], lo[half, :]).then_inc(q_moved[b], 16)
                            else:
                                other = slice(64, 128) if half.start == 0 else slice(0, 64)
                                sp.dma_start(K2[half, ds(h, 1), :], hi[half, :]).then_inc(k_moved[b], 16)
                                sp.dma_start(K2[other, ds(h, 1), :], lo[half, :]).then_inc(k_moved[b], 16)

            for b in range(2):
                sp.sem_inc(k_moved[b], 64)
                sp.sem_inc(q_moved[b], 128)
            sp.wait_ge(spilled, 32)
            sp.wait_ge(zT_done, 4)
            move_heads(FBASE["SPK"], False)
            load(SPO, A["sp_ow"][ds(si, 1)].rearrange("a p k o -> p (a k) o"))
            move_heads(FBASE["SPQ"], True)
            load(TMK, A["tm_w"][ds(ti, 1), 1].rearrange("a p k o -> p (a k) o"))
            load(TMQ, A["tm_w"][ds(ti, 1), 0].rearrange("a p k o -> p (a k) o"))
            sp.wait_ge(accT_free, TBASE["TMV"] + 2)
            sp.dma_start(bb[1][:, :], A["cr_vb"].broadcast_to([TP, D])).then_inc(rows_in["CRV"], 16)
            load(TMV, A["tm_w"][ds(ti, 1), 2].rearrange("a p k o -> p (a k) o"))
            load(TMP, A["tm_w"][ds(ti, 1), 3].rearrange("a p k o -> p (a k) o"))
            move_heads(FBASE["TMK"], False)
            load(CRQ, A["cr_w"][0])
            move_heads(FBASE["TMQ"], True)
            sp.wait_ge(accT_free, TBASE["CRV"] + 2)
            sp.dma_start(bb[0][:, :], A["cr_ob"].broadcast_to([TP, D])).then_inc(rows_in["CRO"], 16)
            load(CRK, A["cr_w"][1])
            load(CRV, A["cr_w"][2])
            move_heads(FBASE["CRQ"], True)
            sp.dma_start(x2, x0_d.rearrange("t p d -> p t d")).then_inc(x0_in, 16)
            move_heads(FBASE["CRK"], False)
            load(CRO, A["cr_ow"])
            sp.wait_ge(accT_free, TBASE["CRO"] + 2)
            sp.dma_start(bb[1][:, :], A["dn_b"].broadcast_to([TP, D])).then_inc(rows_in["DN"], 16)
            for j in range(4):
                load(UP0 + j, A["up_w"][j])
            sp.wait_ge(zT_done, 8)
            sp.dma_start(x1b, x1_d.rearrange("t p d -> p t d")).then_inc(x1_in, 16)
            for j in range(4):
                load(DN0 + j, A["dn_w"][j])
            with sp.Fori(0, NT) as i:
                sp.wait_ge(accT_free, i + (TBASE["DN"] + 3))
                sp.dma_start(out[ds(i * TP, TP), :], x2[:, ds(i, 1), :].rearrange("p a d -> p (a d)")).then_inc(out_done, 16)
            sp.wait_ge(out_done, 16 * NT)

        @block.gpsimd
        def _(pool):
            g = nc.gpsimd
            ds = bass.ds
            n = [0]

            def link(ins):
                n[0] += 1
                ins.then_inc(pool_ch, 1)
                pool.wait_ge(pool_ch, n[0])

            exact = dict(allow_small_or_imprecise_dtypes=True)
            link(g.iota(iota[:, :], [[1, KW]], base=0, channel_multiplier=0, **exact))
            link(g.iota(win25[:, :], [[WIN, NW]], base=0, channel_multiplier=0, **exact))
            link(g.iota(group1[:, :], [[0, 1]], base=1, channel_multiplier=1, **exact))
            link(g.iota(groupr[:, :], [[0, 1]], base=NG, channel_multiplier=-1, **exact))
            link(g.memset(zeros[:, :], 0.0))
            link(g.memset(ident[:, :], 0.0))
            link(g.affine_select(out=ident[:, :], in_=ident[:, :], compare_op=ALU.not_equal, fill=1.0, base=0,
                                 pattern=[[-1, 128]], channel_multiplier=1))
            link(g.memset(ident_b[:, :], 0.0))
            link(g.affine_select(out=ident_b[:, :], in_=ident_b[:, :], compare_op=ALU.not_equal, fill=1.0, base=0,
                                 pattern=[[-1, TP]], channel_multiplier=1))
            link(g.memset(mask[:, :], 0.0))
            link(g.affine_select(out=mask[:, :], in_=mask[:, :], compare_op=ALU.is_ge, fill=MASKED, base=0,
                                 pattern=[[-1, TP]], channel_multiplier=1))
            link(g.iota(rt[0:1, 7, :], [[0, 2], [-1, 4]], base=4, channel_multiplier=0, **exact))
            link(g.memset(kw_col[:, :], float(KW)))
            g.memset(ones[:, :], 1.0).then_inc(consts, 1)

            def split(unit):
                hi, lo = WH[unit % SLOTS], WL[unit % SLOTS]
                pool.wait_ge(w_loaded, 16 * (unit + 1))
                link(g.tensor_scalar(w_in, w_in, WS, 1.0, ALU.mult, ALU.mult))
                link(g.tensor_scalar(hi, w_in, 1.0, 1.0, ALU.mult, ALU.mult))
                link(g.tensor_tensor(lo, w_in, hi, ALU.subtract))
                pool.sem_inc(w_taken, 1)
                pool.sem_inc(w_split, 1)

            pool.wait_ge(xs_scale, 1)
            per = NT * WU // NW

            pool.sem_inc(low_added, 2)

            def add_low(ww, j):
                pool.wait_ge(win_high, ww * WU + (j + 1))
                pool.wait_ge(win_free, ww * WU + (j + 3))
                where = window_adj(ww, j)
                g.tensor_tensor(where, where, low_part[j % 2].rearrange("p (a d) -> p d a", a=NT), ALU.add).then_inc(low_added, 1)

            def scale_xs(tile, col, k, done):
                by = (rstd, nmr)[k][:, col].unsqueeze(2).broadcast_to([TP, 1, D])
                g.tensor_tensor(xs[:, tile, :], xs[:, tile, :], by, (ALU.mult, ALU.add)[k]).then_inc(xs_ready, 1)
                pool.wait_ge(xs_ready, done)

            with pool.Fori(0, NW // WU) as ww:
                for j in range(WU):
                    pool.wait_ge(win_free, ww * WU + (j + 2))
                    pool.wait_ge(krel_ready, ww * WU + (j + 1))
                    g.tensor_tensor(krel[1 - j % 2], krel[j % 2], kw_col[:, 0:1].broadcast_to([TP, EC]),
                                    ALU.subtract).then_inc(krel_ready, 1)
                    add_low(ww, j)
                    if j < 2 * per:
                        at = ds(ww * per + j // 2, 1)
                        scale_xs(at, at, j % 2, (ww * per + j // 2) * 2 + (j % 2 + 1))
            add_low(NW // WU, 0)
            for t in range(NW // WU * per, NT):
                for k in range(2):
                    scale_xs(slice(t, t + 1), slice(t, t + 1), k, 2 * t + k + 1)
            def attention(a):
                S = att[a]

                def output(T, it):
                    pool.wait_ge(S["oT_hi"], T + it * PER2["tile"])
                    cols = tile_columns(T - 1, it)
                    g.tensor_tensor(at_[1][:, :, cols], oT, at_[0][:, :, cols], ALU.subtract).then_inc(S["oT_lo"], 1)

                def body(T, it):
                    for h in range(H):
                        if h == 3 and T >= 1:
                            output(T, it)
                        for c, (c0, c1) in enumerate(chunks(a, T)):
                            wait_split(pool, a, "hi", T, h, c, it, 1)
                            if c == 0 and T * H + h >= 2:
                                pool.wait_ge(S["av_done"], T * H + h - 1 + it * PER2["step"])
                            g.tensor_tensor(pT_lo[h % 2][:, c0:c1, :], probT[:, c0:c1, :], pT_hi[h % 2][:, c0:c1, :],
                                            ALU.subtract).then_inc(S[f"lo_{c}"], 1)

                attention_tiles(pool, a, body)
                output(NT, 0)

            split(LIN)
            pool.wait_ge(xr_in, 16)
            pool.wait_ge(linb_in, 16)
            for t in range(NT):
                last = g.tensor_tensor(xb[:, t, :], xb[:, t, :], bb[0][:, :], ALU.add)
            link(last)
            pool.sem_inc(xb_ready, 1)
            pool.wait_ge(accF_done, FBASE["SPK"])
            split(SPK)
            split(SPQ)
            split(SPV)
            pool.wait_ge(accT_done, TBASE["SPV"])
            split(SPO)
            attention(0)
            pool.wait_ge(accF_done, FBASE["SPK"] + 4)
            split(TMK)
            pool.wait_ge(accF_done, FBASE["SPQ"] + 4)
            split(TMQ)
            pool.wait_ge(accT_done, TBASE["SPV"] + NT)
            split(TMV)
            pool.wait_ge(accF_done, FBASE["SPO"] + 4)
            split(TMP)
            attention(1)
            pool.wait_ge(accF_done, FBASE["TMK"] + 4)
            split(CRQ)
            pool.wait_ge(accF_done, FBASE["TMQ"] + 4)
            split(CRK)
            pool.wait_ge(accT_done, TBASE["TMV"] + NT)
            split(CRV)
            pool.wait_ge(accF_done, FBASE["TMP"] + 4)
            split(CRO)
            pool.wait_ge(x0_in, 16)
            pool.wait_ge(rows_in["CRO"], 16)
            for t in range(NT):
                last = g.tensor_tensor(x2[:, t, :], x2[:, t, :], bb[0][:, :], ALU.add)
            link(last)
            pool.sem_inc(x0b_ready, 1)
            attention(2)
            pool.wait_ge(accF_done, FBASE["CRQ"] + 4)
            split(UP0)
            pool.wait_ge(accF_done, FBASE["CRK"] + 4)
            split(UP0 + 1)
            pool.wait_ge(accT_done, TBASE["CRV"] + NT)
            split(UP0 + 2)
            pool.wait_ge(accT_done, TBASE["CRO"] + NT)
            split(UP0 + 3)
            pool.wait_ge(x1_in, 16)
            pool.wait_ge(rows_in["DN"], 16)
            for t in range(NT):
                link(g.tensor_tensor(x1b[:, t, :], x1b[:, t, :], bb[1][:, :], ALU.add))
                last = g.tensor_tensor(x2[:, t, :], x2[:, t, :], x1b[:, t, :], ALU.add)
            link(last)
            pool.sem_inc(x1b_ready, 1)
            for j in range(4):
                pool.wait_ge(accF_done, FBASE[f"UP{j}"] + 4)
                split(DN0 + j)

        @block.tensor
        def _(pe):
            mm_ = nc.tensor.matmul
            ds = bass.ds
            pe.wait_ge(consts, 1)
            pe.wait_ge(bounds_ready, 1)
            nc.tensor.transpose(PS[0:2 * NW, 0:NG], win_v, ident[0:NG, 0:NG]).then_inc(boundsT, 1)
            pe.wait_ge(rmax_ready, 1)
            mm_(PS[0:1, 512:512 + 2 * NW], rmax[:, :], ident[0:2 * NW, 0:2 * NW], start=True, stop=True).then_inc(rows_done, 1)

            pe.wait_ge(hi_ready, 1)
            DEG = PS[0:3 * NT, 1024:1024 + 3 * TP]
            mm_(DEG, zeros[:, 0:3 * NT], iota[:, 0:1].broadcast_to([TP, 3 * TP]), start=True, stop=False)
            for part in range(HOT_PARTS):
                pe.wait_ge(lo_ready, part + 1)
                with pe.Fori(2 * part, 2 * part + 2) as j:
                    for c in range(0, EC // HOT_PARTS // 2, 3):
                        at = ds(j * (EC // HOT_PARTS // 2) + c, 3)
                        last = mm_(DEG, hi_hot[:, at, :], lo_hot[:, at, :], start=False, stop=False)
            mm_(DEG, zeros[:, 0:3 * NT], iota[:, 0:1].broadcast_to([TP, 3 * TP]), start=False, stop=True).then_inc(deg_done, 1)
            pe.wait_ge(deg3_ready, 1)
            for c in range(3):
                last = nc.tensor.transpose(PS[0:TP, 1536 + 3 * NT * c:1536 + 3 * NT * (c + 1)], deg3[:, c * TP:(c + 1) * TP],
                                           ident[0:3 * NT, 0:3 * NT])
            last.then_inc(deg_done, 1)

            pe.wait_ge(visits_ready, 1)
            for g in range(GC):
                pe.sem_inc(hot_free[g], 1)
            pe.sem_inc(win_free, 2)

            def window_acc(j, half):
                at = 2048 + 1024 * (j % 2) + 512 * half
                return PS[0:TP, at:at + KW]

            def open_window(ww, j):
                pe.wait_ge(win_free, ww * WU + (j + 1))
                for half in range(2):
                    mm_(window_acc(j, half), zeros[:, :], iota[:, :], start=True, stop=False)

            def close_window(ww, j):
                for half in range(2):
                    last = mm_(window_acc(j, half), zeros[:, :], iota[:, :], start=False, stop=True)
                last.then_inc(win_done, 1)

            def add_group(j, visit, group):
                for g in range(GC):
                    pe.wait_ge(key_made[g], visit + 1)
                    mm_(window_acc(j, 0), lo_hot[:, ds(group * GC + g, 1), :], key_hot[:, g, :], start=False, stop=False)
                    pe.wait_ge(low_made[g], visit + 1)
                    mm_(window_acc(j, 1), low_hot[:, g, :], key_hot[:, g, :], start=False, stop=False).then_inc(hot_free[g], 1)

            windows(pe, add_group, open_window, close_window)

            pe.wait_ge(xs_ready, 2 * NT)
            pe.wait_ge(low_added, NW + 2)
            for m in range(KD):
                base = (m % 2) * ACC
                if m >= 2:
                    pe.wait_ge(accF_read, m - 1 + 2)
                for s, e in SPLITS:
                    for k in range(NT):
                        last = mm_(PS[:, base + s:base + e], xs[:, k, m * 128:(m + 1) * 128], adj[:, k, s:e],
                                   start=(k == 0), stop=(k == NT - 1))
                last.then_inc(accF_done, 1)

            def feature_product(name, unit, x, kt0=0):
                f = FBASE[name]
                hi, lo = WH[unit % SLOTS], WL[unit % SLOTS]
                pe.wait_ge(w_split, unit + 1)
                with pe.Fori(0, 2) as mm:
                    for b in range(2):
                        m = mm * 2 + b
                        pe.wait_ge(accF_read, m + (f + 1))
                        for k in range(KD):
                            for i, (w, v) in enumerate(((hi, x[0]), (hi, x[1]), (lo, x[0]))):
                                for s, e in SPLITS:
                                    last = mm_(PS[:, b * ACC + s:b * ACC + e], w[:, k, ds(m * 128, 128)], v[:, k, s:e],
                                               start=(k == 0 and i == 0), stop=(k == KD - 1 and i == 2))
                        last.then_inc(accF_done, 1)

            def token_product(name, units, x):
                t0 = TBASE[name]
                pe.wait_ge(w_split, units[-1] + 1)
                with pe.Fori(0, NT // 2) as ii:
                    for b in range(2):
                        i = ii * 2 + b
                        pe.wait_ge(accT_free, i + (t0 + 1))
                        for u, unit in enumerate(units):
                            hi, lo = WH[unit % SLOTS], WL[unit % SLOTS]
                            for k in range(KD):
                                for j, (v, w) in enumerate(((x[0], hi), (x[0], lo), (x[1], hi))):
                                    last = mm_(PS[0:TP, b * ACC:b * ACC + D], v[:, u * KD + k, ds(i * TP, TP)], w[:, k, :],
                                               start=(u == 0 and k == 0 and j == 0),
                                               stop=(u == len(units) - 1 and k == KD - 1 and j == 2))
                        last.then_inc(accT_done, 1)

            pe.wait_ge(y_split, FBASE["agg"] + 4 + 2)
            pe.wait_ge(accF_read, FBASE["SPK"] + 2)
            token_product("LIN", [LIN], agg)

            pe.wait_ge(x0_ready, 2)
            for k in range(KD):
                for t in range(NT):
                    last = mm_(PS[:, T_BANK + k:T_BANK + k + 1], x0[:, t, k * 128:(k + 1) * 128], ones[:, :],
                               start=(t == 0), stop=(t == NT - 1))
            last.then_inc(r_pool, 1)
            pe.wait_ge(rw_in, 16)
            pe.wait_ge(r_poolc, 1)
            for k in range(KD):
                last = mm_(PS[:, O_BANK:O_BANK + 1], rw1[:, k, :], pooled[:, k:k + 1], start=(k == 0), stop=(k == KD - 1))
            last.then_inc(r_hid, 1)
            pe.wait_ge(cols_in, 16 * 6)
            pe.wait_ge(r_gelu, 1)
            mm_(PS[0:1, T_BANK:T_BANK + 8], hid[:, :], rw2[:, :], start=True, stop=True).then_inc(r_log, 1)

            def to_features(z, done_before):
                for m in range(KD):
                    if m >= 2:
                        pe.wait_ge(zT_act, done_before + m - 1)
                        pe.wait_ge(zT_dve, done_before + m - 1)
                    for t in range(NT):
                        at0 = (m % 2) * ACC + (t // 4) * 512 + (t % 4) * TP
                        last = nc.tensor.transpose(PS[:, at0:at0 + TP], z[:, t, m * 128:(m + 1) * 128], ident[0:TP, 0:TP])
                    last.then_inc(zT_done, 1)

            pe.wait_ge(z0_ready, 1)
            pe.wait_ge(accT_free, TBASE["SPV"] + 2)
            to_features(z0, 0)

            def attention(a, causal):
                S = att[a]

                def scores(T, h, it, chunk):
                    width = TP * key_tiles(a, T)
                    nch = (width + 511) // 512
                    if chunk >= nch:
                        return
                    b = h % 2
                    s, e = chunk * 512, min(chunk * 512 + 512, width)
                    acc = PS[0:TP, b * ACC + s:b * ACC + e]
                    qs = ds(it * (2 * TP) + T * TP, TP) if not isinstance(it, int) else slice(T * TP, (T + 1) * TP)
                    diag = (max(s, T * TP), min(e, (T + 1) * TP))
                    masked = causal and diag[0] < diag[1]
                    mm_(acc, QA[:, h, qs], K2[:, h, s:e], start=True, stop=False)
                    last = mm_(acc, QB[:, h, qs], K2[:, h, s:e], start=False, stop=not masked)
                    if masked:
                        last = mm_(PS[0:TP, b * ACC + diag[0]:b * ACC + diag[1]], ident_b[:, :],
                                   mask[:, diag[0] - T * TP:diag[1] - T * TP], start=False, stop=True)
                    if chunk == nch - 1:
                        last.then_inc(S["s_done"], 1)

                def transposes(T, h, it, c):
                    cs = chunks(a, T)
                    if c >= len(cs):
                        return
                    turn = t_before(a, T, h, c)
                    if c < 2 and turn:
                        pe.wait_ge(S["t_free"], turn + it * PER2["turn"])
                    for kt in range(*cs[c]):
                        o = (T_BANK if c < 2 else third_group(h)) + (kt - cs[c][0]) * TP
                        last = nc.tensor.transpose(PS[0:TP, o:o + TP], prob[h % 2][:, kt * TP:(kt + 1) * TP], ident[0:TP, 0:TP])
                    last.then_inc(S["t_full" if c < 2 else "t2_full"], 1)

                def values(T, h, it, part):
                    n_ = key_tiles(a, T)
                    if part == 0 and h % 4 == 0 and (T or h):
                        pe.wait_ge(S["o_read"], 2 * T + h // 4 + it * PER2["half"])
                    last = None
                    for kt in (range(min(AV_FIRST, n_)) if part == 0 else range(AV_FIRST, n_)):
                        if kt % 4 == 0:
                            wait_split(pe, a, "hi", T, h, kt // 4, it, 1)
                            wait_split(pe, a, "lo", T, h, kt // 4, it, 1)
                        for half in (pT_hi, pT_lo):
                            last = mm_(PS[0:TP, O_BANK + (h % 4) * 2 * HD:O_BANK + (h % 4 + 1) * 2 * HD], half[h % 2][:, kt, :],
                                       V[:, kt, h, :], start=(kt == 0 and half is pT_hi), stop=(kt == n_ - 1 and half is pT_lo))
                    if last and kt == n_ - 1:
                        last.then_inc(S["av_done"], 1)

                def output(T, it):
                    turn = t_before(a, T, 3, 0) - 1 if T < NT else t_before(a, NT - 1, H - 1, len(chunks(a, NT - 1)))
                    pe.wait_ge(S["t_free"], turn + it * PER2["turn"])
                    pe.wait_ge(S["o_ready"], 2 * T + it * PER2["half"])
                    for k in range(KD):
                        last = nc.tensor.transpose(PS[:, T_BANK + k * TP:T_BANK + (k + 1) * TP],
                                                   otok[(T - 1) % 2][:, k * 128:(k + 1) * 128], ident[0:TP, 0:TP])
                    last.then_inc(S["t_full"], 1)

                def body(T, it):
                    for h in range(H):
                        later = [(T, h + d) if h + d < H else (T + 1, h + d - H) for d in range(4)]
                        before = (T, h - 1) if h else (T - 1, H - 1)
                        transposes(T, h, it, 0)
                        if later[2][0] < NT:
                            scores(*later[2], it, 1)
                            if c_before(a, T, h, 2) > 0:
                                pe.wait_ge(S["t2_free"], c_before(a, T, h, 2) + it * PER2["step"])
                            scores(*later[2], it, 2)
                        if T or h:
                            values(*before, it, 0)
                        transposes(T, h, it, 1)
                        if T or h:
                            values(*before, it, 1)
                        if h == 2 and T >= 1:
                            output(T, it)
                        if later[1][0] < NT:
                            pe.wait_ge(S["exp_done"], T * H + h + 2 + it * PER2["step"])
                        transposes(T, h, it, 2)
                        if later[3][0] < NT:
                            scores(*later[3], it, 0)

                for h in range(2):
                    for c in range(3):
                        scores(0, h, 0, c)
                pe.wait_ge(S["exp_done"], 1)
                scores(0, 2, 0, 0)
                attention_tiles(pe, a, body)
                values(NT - 1, H - 1, 0, 0)
                values(NT - 1, H - 1, 0, 1)
                output(NT, 0)

            def stage_clear(f, t):
                pe.wait_ge(accF_read, f + 2)
                pe.wait_ge(accT_free, t + 2)

            FB, TB = FBASE, TBASE
            pe.wait_ge(y_split, FB["SPK"] + 2)
            pe.wait_ge(zT_act, 4)
            pe.wait_ge(zT_dve, 4)
            feature_product("SPK", SPK, xn)
            feature_product("SPQ", SPQ, xn)
            stage_clear(FB["SPO"], TB["SPV"])
            token_product("SPV", [SPV], xn)
            stage_clear(FB["SPO"], TB["TMV"])
            heads_moved(pe, 1)
            attention(0, False)
            pe.wait_ge(att[0]["oT_lo"], NT)
            feature_product("SPO", SPO, at_)
            feature_product("TMK", TMK, xt)
            feature_product("TMQ", TMQ, xt)
            stage_clear(FB["TMP"], TB["TMV"])
            token_product("TMV", [TMV], xt)
            stage_clear(FB["TMP"], TB["CRV"])
            heads_moved(pe, 2)
            attention(1, True)
            pe.wait_ge(att[1]["oT_lo"], NT)
            feature_product("TMP", TMP, at_)
            feature_product("CRQ", CRQ, so)
            pe.wait_ge(y_split, FB["TMP"] + 4 + 2)
            feature_product("CRK", CRK, to)
            stage_clear(FB["UP0"], TB["CRV"])
            token_product("CRV", [CRV], to)
            stage_clear(FB["UP0"], TB["CRO"])
            heads_moved(pe, 3)
            attention(2, False)
            pe.wait_ge(att[2]["oT_lo"], NT)
            token_product("CRO", [CRO], at_)
            pe.wait_ge(z2_ready, 1)
            to_features(z2, 4)
            pe.wait_ge(zT_act, 8)
            pe.wait_ge(zT_dve, 8)
            for j in range(4):
                feature_product(f"UP{j}", UP0 + j, h2)
            pe.wait_ge(y_split, FB["UP3"] + 4 + 2)
            stage_clear(FB["UP3"] + 4, TB["DN"])
            token_product("DN", [DN0 + j for j in range(4)], gT)

        @block.scalar
        def _(act):
            a_ = nc.scalar.activation
            ds = bass.ds
            act.dma_start(confw[:, :], A["conf"].broadcast_to([TP, 4])).then_inc(conf_in, 16)
            act.dma_start(bb[0][:, :], A["lin_b"].broadcast_to([TP, D])).then_inc(linb_in, 16)
            act.dma_start(norms[:, :, :], A["norms"]).then_inc(cols_in, 16)
            act.dma_start(cr_b[:, :, :], A["cr_qkb"]).then_inc(cols_in, 16)
            act.dma_start(up_b[:, :], A["up_b"]).then_inc(cols_in, 16)
            act.dma_start(rw2[:, :], A["r_w2"]).then_inc(cols_in, 16)
            act.dma_start(rb1[:, :], A["r_b1"]).then_inc(cols_in, 16)
            act.dma_start(rb2[:, :], A["r_b2"]).then_inc(cols_in, 16)
            act.wait_ge(conf_in, 16)
            act.wait_ge(logit_ready, 1)
            a_(ew, ew, ACT.Sigmoid, bias=confw[:, 3:4]).then_inc(ew_ready, 1)

            roots = [0]

            def root(dst, src):
                roots[0] += 1
                act.wait_ge(var_ready, roots[0])
                a_(dst, src, ACT.Sqrt).then_inc(std_ready, 1)

            root(rstd[:, :], rstd[:, :])
            root(dis[:, :], dis[:, :])
            act.wait_ge(visits_ready, 1)

            def low_halves(j, visit, group):
                for g in range(GC):
                    act.wait_ge(hot_free[g], visit + 1)
                    c = ds(group * GC + g, 1)
                    a_(low_hot[:, g, :].unsqueeze(1), lo_hot[:, c, :], ACT.Copy, scale=w_ratio[:, c]).then_inc(low_made[g], 1)

            def read_window(ww, j):
                act.wait_ge(win_done, ww * WU + (j + 1))
                at = 2048 + 1024 * (j % 2)
                a_(window_adj(ww, j), PS[0:TP, at:at + KW].rearrange("p (d a) -> p d a", a=NT),
                   ACT.Copy, scale=1.0 / ES).then_inc(win_high, 1)
                act.wait_ge(low_added, ww * WU + (j + 1))
                a_(low_part[j % 2].rearrange("p (a d) -> p d a", a=NT), PS[0:TP, at + 512:at + 512 + KW].rearrange("p (d a) -> p d a", a=NT),
                   ACT.Copy, scale=1.0 / (ES * LS)).then_inc(win_free, 1)

            windows(act, low_halves, None, read_window)

            act.sem_inc(accF_read, 2)

            def read_features(name, bias, scale=1.0 / WS, fn=ACT.Identity):
                f = FBASE[name]
                with act.Fori(0, 2) as mm:
                    for b in range(2):
                        m = mm * 2 + b
                        act.wait_ge(accF_done, m + (f + 1))
                        act.wait_ge(y_split, m + (f + 1))
                        extra = {} if bias is None else {"bias": bias[:, ds(m, 1)]}
                        a_(y32[b], PS[:, b * ACC:b * ACC + N], fn, scale=scale, **extra).then_inc(accF_read, 1)

            read_features("agg", None, scale=1.0)
            root(rstd[:, :], rstd[:, :])
            root(rstd[:, :], rstd[:, :])
            act.wait_ge(cols_in, 16 * 6)
            act.wait_ge(r_hid, 1)
            a_(hid[:, :], PS[:, O_BANK:O_BANK + 1], ACT.Gelu, bias=rb1[:, :]).then_inc(r_gelu, 1)
            act.wait_ge(r_max, 1)
            a_(rt[0:1, 1, :], rt[0:1, 0, :], ACT.Exp, bias=rt[0:1, 2, 0:1], accum_out=rt[0:1, 2, 1:2]).then_inc(r_exp, 1)

            def scaled_features(base, weight, bias):
                for m in range(KD):
                    b = m % 2
                    act.wait_ge(zT_done, base + m + 1)
                    if m >= 2:
                        act.wait_ge(zT_dve, base + m - 1)
                    for s, w_ in ((0, 1000), (1000, 250)):
                        src = PS[:, b * ACC + (s // 500) * 512:b * ACC + (s // 500) * 512 + 1024 if s == 0 else b * ACC + 1024 + 250]
                        if s == 0:
                            src = src.rearrange("p (c n) -> p c n", n=512)[:, :, 0:500]
                            dst = y32[b][:, 0:1000].rearrange("p (c n) -> p c n", n=500)
                        else:
                            dst = y32[b][:, 1000:1250]
                        last = a_(dst, src, ACT.Identity, scale=norms[:, weight, m:m + 1], bias=norms[:, bias, m:m + 1])
                    last.then_inc(zT_act, 1)

            act.wait_ge(cols_in, 16 * 6)
            act.wait_ge(y_split, FBASE["agg"] + 4 + 2)
            scaled_features(0, 0, 1)
            act.wait_ge(qb_ready, 1)
            act.wait_ge(zT_dve, 4)
            read_features("SPK", sp_b[:, 0, :])
            read_features("SPQ", q_b[:, 0, :], scale=0.125 / WS)

            def attention(a):
                S = att[a]

                def exps(T, h, it):
                    if T >= NT:
                        return
                    act.wait_ge(S["max_done"], T * H + h + 1 + it * PER2["step"])
                    done = t_before(a, *((T, h - 1) if h else (T - 1, H - 1)), 0) if (T or h) else 0
                    if T * H + h >= 2:
                        act.wait_ge(S["t_full"], done + it * PER2["turn"])
                        c2 = c_before(a, *((T, h - 1) if h else (T - 1, H - 1)), 2)
                        if c2 > 0:
                            act.wait_ge(S["t2_full"], c2 + it * PER2["step"])
                    n_ = TP * key_tiles(a, T)
                    a_(prob[h % 2][:, 0:n_], PS[0:TP, (h % 2) * ACC:(h % 2) * ACC + n_], ACT.Exp, bias=nmax[:, h % 2:h % 2 + 1],
                       accum_out=rsum[:, T % 2, h:h + 1]).then_inc(S["exp_done"], 1)

                def output(T, it):
                    turn = t_before(a, T, 3, 0) if T < NT else t_before(a, NT - 1, H - 1, len(chunks(a, NT - 1))) + 1
                    act.wait_ge(S["t_full"], turn + it * PER2["turn"])
                    if T > 1:
                        act.wait_ge(S["oT_lo"], T - 1 + it * PER2["tile"])
                    a_(oT, PS[:, T_BANK:T_BANK + KD * TP].rearrange("p (k n) -> p k n", n=TP), ACT.Copy).then_inc(S["t_free"], 1)
                    act.wait_ge(S["t_free"], turn + it * PER2["turn"])
                    a_(at_[0][:, :, tile_columns(T - 1, it)], oT, ACT.Copy).then_inc(S["oT_hi"], 1)

                def high(T, h, it, c):
                    c0, c1 = chunks(a, T)[c]
                    act.wait_ge(S["t_free"], t_before(a, T, h, c + 1) + it * PER2["turn"])
                    if T * H + h >= 2:
                        act.wait_ge(S["av_done"], T * H + h - 1 + it * PER2["step"])
                    a_(pT_hi[h % 2][:, c0:c1, :], probT[:, c0:c1, :], ACT.Copy).then_inc(S[f"hi_{c}"], 1)

                def body(T, it):
                    for h in range(H):
                        exps(*((T, h + 1) if h + 1 < H else (T + 1, 0)), it)
                        high(T, h, it, 0)
                        if len(chunks(a, T)) > 1:
                            act.wait_ge(S["t_full"], t_before(a, T, h, 2) + it * PER2["turn"])
                            wait_split(act, a, "lo", T, h, 1, it, 0)
                            c0, c1 = chunks(a, T)[1]
                            a_(probT[:, c0:c1, :],
                               PS[0:TP, T_BANK:T_BANK + (c1 - c0) * TP].rearrange("p (k n) -> p k n", n=TP),
                               ACT.Copy).then_inc(S["t_free"], 1)
                            high(T, h, it, 1)
                        if h == 2 and T >= 1:
                            output(T, it)

                exps(0, 0, 0)
                attention_tiles(act, a, body)
                output(NT, 0)

            attention(0)
            read_features("SPO", sp_ob)
            act.wait_ge(tmb_in, 16)
            read_features("TMK", tm_b[:, 0, :])
            read_features("TMQ", q_b[:, 1, :], scale=0.125 / WS)
            attention(1)
            read_features("TMP", tm_b[:, 2, :])
            read_features("CRQ", q_b[:, 2, :], scale=0.125 / WS)
            read_features("CRK", cr_b[:, 1, :])
            attention(2)
            root(rstd[:, :], rstd[:, :])
            scaled_features(4, 4, 5)
            act.wait_ge(zT_dve, 8)
            for j in range(4):
                read_features(f"UP{j}", up_b[:, 4 * j:4 * j + 4], fn=ACT.Gelu)

        @block.vector
        def _(dve):
            v = nc.vector
            ds = bass.ds
            n = [0]

            def link(ins):
                n[0] += 1
                ins.then_inc(dve_ch, 1)
                dve.wait_ge(dve_ch, n[0])

            dve.wait_ge(edges_in, 64)
            dve.wait_ge(consts, 1)
            v.tensor_reduce(dmm[:, 0:1], dst_g, AX.X, ALU.min)
            link(v.tensor_reduce(dmm[:, 1:2], dst_g, AX.X, ALU.max))
            link(v.tensor_scalar(dmm[:, 0:1], dmm[:, 0:1], float(1 - WIN), None, ALU.add))
            link(v.tensor_scalar(win_t, win25, dmm[:, 0:1], None, ALU.is_ge))
            link(v.scalar_tensor_tensor(win_t, win25, dmm[:, 1:2], win_t, ALU.is_le, ALU.mult))
            v.tensor_scalar(win_v[:, 0:NW], win_t, group1[:, 0:1], None, ALU.mult)
            v.tensor_scalar(win_v[:, NW:2 * NW], win_t, groupr[:, 0:1], None, ALU.mult).then_inc(bounds_ready, 1)
            dve.wait_ge(conf_in, 16)
            link(v.tensor_scalar(ew, attr[:, 0, :], confw[:, 0:1], None, ALU.mult))
            link(v.scalar_tensor_tensor(ew, attr[:, 1, :], confw[:, 1:2], ew, ALU.mult, ALU.add))
            v.scalar_tensor_tensor(ew, attr[:, 2, :], confw[:, 2:3], ew, ALU.mult, ALU.add).then_inc(logit_ready, 1)
            link(v.tensor_copy(src_f, src_i))
            link(v.tensor_scalar(src_hi, src_f, float(TP), None, ALU.is_ge))
            for t in range(2, NT):
                link(v.scalar_tensor_tensor(src_hi, src_f, float(TP * t), src_hi, ALU.is_ge, ALU.add))
            link(v.scalar_tensor_tensor(src_lo, src_hi, float(-TP), src_f, ALU.mult, ALU.add))
            v.scalar_tensor_tensor(krel[0], dst_i, float(NT), src_hi, ALU.mult, ALU.add).then_inc(krel_ready, 1)
            v.tensor_tensor(hi_hot, src_hi.unsqueeze(2).broadcast_to([TP, EC, NT]),
                            iota[:, 0:NT].unsqueeze(1).broadcast_to([TP, EC, NT]), ALU.is_equal).then_inc(hi_ready, 1)

            def source_hots(part):
                n_ = EC // HOT_PARTS
                c = slice(part * n_, (part + 1) * n_)
                v.tensor_tensor(lo_hot[:, c, :], src_lo[:, c].unsqueeze(2).broadcast_to([TP, n_, TP]),
                                iota[:, 0:TP].unsqueeze(1).broadcast_to([TP, n_, TP]), ALU.is_equal).then_inc(lo_ready, 1)

            source_hots(0)
            dve.wait_ge(boundsT, 1)
            v.tensor_reduce(rmax[:, :], PS[0:2 * NW, 0:NG], AX.X, ALU.max).then_inc(rmax_ready, 1)

            def window_table():
                dve.wait_ge(rows_done, 1)
                link(v.tensor_scalar(rows[0:1, 0, 0:NW], PS[0:1, 512 + NW:512 + 2 * NW], -1.0, float(NG), ALU.mult, ALU.add))
                link(v.tensor_scalar(rows[0:1, 0, 0:NW], rows[0:1, 0, 0:NW], float(NG - 1), None, ALU.min))
                link(v.scalar_tensor_tensor(rows[0:1, 1, 0:NW], rows[0:1, 0, 0:NW], 1.0, PS[0:1, 512:512 + NW], ALU.add, ALU.max))
                link(v.tensor_tensor(rows[0:1, 2, 0:NW], rows[0:1, 1, 0:NW], rows[0:1, 0, 0:NW], ALU.subtract))
                cur, step = 2, 1
                while step < NW:
                    other = {2: 3, 3: 1, 1: 3}[cur]
                    v.tensor_copy(rows[0:1, other, 0:step], rows[0:1, cur, 0:step])
                    link(v.tensor_tensor(rows[0:1, other, step:NW], rows[0:1, cur, step:NW], rows[0:1, cur, 0:NW - step], ALU.add))
                    cur, step = other, step * 2
                v.tensor_copy(visits[0:1, 0:1], rows[0:1, 0, 0:1])
                v.scalar_tensor_tensor(visits[0:1, 1:NW], rows[0:1, cur, 0:NW - 1], float(PACK), rows[0:1, 0, 1:NW], ALU.mult, ALU.add)
                v.tensor_scalar(visits[0:1, NW:NW + 1], rows[0:1, cur, NW - 1:NW], float(PACK), None, ALU.mult).then_inc(visits_ready, 1)

            def statistics(x):
                for t in range(NT):
                    last = v.bn_stats(stat[:, t, :], x[:, t, :])
                link(last)
                for t in range(NT):
                    last = v.bn_aggr(mv[:, t, :], stat[:, t, :])
                link(last)
                link(v.tensor_scalar(var[:, :], mv[:, :, 1], EPS, None, ALU.add))
                v.tensor_copy(rstd[:, :], var[:, :]).then_inc(var_ready, 1)

            def inverse_root(y, x):
                link(v.reciprocal(y, y))
                link(v.tensor_tensor(newton[:, :], y, y, ALU.mult))
                link(v.tensor_tensor(newton[:, :], newton[:, :], x, ALU.mult))
                link(v.tensor_scalar(newton[:, :], newton[:, :], -0.5, 1.5, ALU.mult, ALU.add))
                link(v.tensor_tensor(y, y, newton[:, :], ALU.mult))

            dve.wait_ge(x_in, 16)
            statistics(xs)
            source_hots(1)
            source_hots(2)
            dve.wait_ge(std_ready, 1)
            inverse_root(rstd[:, :], var[:, :])
            source_hots(3)
            source_hots(4)
            dve.wait_ge(ew_ready, 1)
            link(v.tensor_scalar(ew, ew, 0.0, ES, ALU.max, ALU.mult))
            link(v.tensor_copy(w16, ew))
            link(v.tensor_copy(w_hi, w16))
            link(v.tensor_tensor(w_lo, ew, w_hi, ALU.subtract))
            link(v.tensor_scalar(w_ratio, w_hi, 1e-30, None, ALU.max))
            link(v.reciprocal(w_ratio, w_ratio))
            link(v.scalar_tensor_tensor(w_ratio, w_ratio, LS, w_lo, ALU.mult, ALU.mult))
            dve.wait_ge(deg_done, 1)
            v.tensor_copy(deg3[:, :], PS[0:3 * NT, 1024:1024 + 3 * TP]).then_inc(deg3_ready, 1)
            window_table()
            dve.wait_ge(deg_done, 2)
            at = [1536 + (3 * NT + NT) * c for c in range(3)]
            link(v.tensor_copy(deg[:, :], PS[0:TP, at[0]:at[0] + NT]))
            for c in (1, 2):
                link(v.tensor_tensor(deg[:, :], deg[:, :], PS[0:TP, at[c]:at[c] + NT], ALU.add))
            link(v.tensor_scalar(dis_s[:, :], deg[:, :], 0.0, None, ALU.is_gt))
            link(v.tensor_scalar(deg[:, :], deg[:, :], 1.0, None, ALU.max))
            v.tensor_copy(dis[:, :], deg[:, :]).then_inc(var_ready, 1)
            dve.wait_ge(std_ready, 2)
            inverse_root(dis[:, :], deg[:, :])
            link(v.tensor_tensor(dis[:, :], dis[:, :], dis_s[:, :], ALU.mult))
            link(v.tensor_tensor(rstd[:, :], rstd[:, :], dis[:, :], ALU.mult))
            v.tensor_scalar(dis_s[:, :], dis[:, :], 1.0 / WS, None, ALU.mult)
            v.scalar_tensor_tensor(nmr[:, :], mv[:, :, 0], -1.0, rstd[:, :], ALU.mult, ALU.mult).then_inc(xs_scale, 1)

            dve.wait_ge(visits_ready, 1)

            def key_hots(j, visit, group):
                for g in range(GC):
                    dve.wait_ge(hot_free[g], visit + 1)
                    c = ds(group * GC + g, 1)
                    v.tensor_scalar(key_hot[:, g, :], iota[:, :], krel[j % 2][:, c], w_hi[:, c],
                                    ALU.is_equal, ALU.mult).then_inc(key_made[g], 1)

            windows(dve, key_hots, lambda ww, j: dve.wait_ge(krel_ready, ww * WU + (j + 1)))

            dve.wait_ge(krel_ready, NW)
            dve.sem_inc(y_split, 2)
            dve.sem_inc(accT_free, 2)

            def split_features(name, dst, moved=None, moved_base=0, per=0, add=None, off=0):
                f = FBASE[name]
                with dve.Fori(0, 2) as mm:
                    for b in range(2):
                        m = mm * 2 + b
                        dve.wait_ge(accF_read, m + (f + 1 + 2))
                        if dst is None:
                            dve.wait_ge(moved[b], mm * per + (moved_base + per))
                            hi, lo = part_hi[b].unsqueeze(1), part_lo[b].unsqueeze(1)
                        else:
                            hi, lo = dst[0][:, ds(m + off, 1), :], dst[1][:, ds(m + off, 1), :]
                        y = y32[b].unsqueeze(1)
                        if add is not None:
                            for p in add:
                                v.tensor_tensor(y, y, p[:, ds(m, 1), :], ALU.add).then_inc(res_done, 1)
                                dve.wait_ge(res_done, m * 2 + (1 if p is add[0] else 2))
                        v.tensor_scalar(hi, y, 1.0, None, ALU.mult).then_inc(hi_done, 1)
                        dve.wait_ge(hi_done, m + (f + 1))
                        v.tensor_tensor(lo, y, hi, ALU.subtract).then_inc(y_split, 1)

            split_features("agg", agg)
            dve.wait_ge(xb_ready, 1)
            for i in range(NT):
                dve.wait_ge(accT_done, TBASE["LIN"] + i + 1)
                last = v.scalar_tensor_tensor(x1[:, i, :], PS[0:TP, (i % 2) * ACC:(i % 2) * ACC + D], dis_s[:, i:i + 1], xb[:, i, :],
                                              ALU.mult, ALU.add)
                last.then_inc(accT_free, 1)
            dve.wait_ge(accT_free, NT + 2)

            def normalised(dst, x, root_no):
                statistics(x)
                dve.wait_ge(std_ready, root_no)
                inverse_root(rstd[:, :], var[:, :])
                for t in range(NT):
                    last = v.tensor_scalar(dst[:, t, :], x[:, t, :], mv[:, t, 0:1], rstd[:, t:t + 1], ALU.subtract, ALU.mult)
                return last

            dve.sem_inc(x0_ready, 1)
            link(normalised(x0, x1, 3))
            dve.sem_inc(x0_ready, 1)
            normalised(z0, x0, 4).then_inc(z0_ready, 1)
            dve.wait_ge(r_pool, 1)
            v.tensor_scalar(pooled[:, :], PS[:, T_BANK:T_BANK + KD], 1.0 / N, None, ALU.mult).then_inc(r_poolc, 1)
            dve.wait_ge(cols_in, 16 * 6)
            dve.wait_ge(r_log, 1)
            link(v.tensor_tensor(rt[0:1, 0, :], PS[0:1, T_BANK:T_BANK + 8], rb2[:, :], ALU.add))
            v.tensor_reduce(rt[0:1, 2, 0:1], rt[0:1, 0, :], AX.X, ALU.max, negate=True).then_inc(r_max, 1)
            dve.wait_ge(r_exp, 1)
            link(v.reciprocal(rt[0:1, 2, 2:3], rt[0:1, 2, 1:2]))
            link(v.tensor_scalar(rt[0:1, 1, :], rt[0:1, 1, :], rt[0:1, 2, 2:3], None, ALU.mult))
            link(v.tensor_reduce(rt[0:1, 3, 0:2], rt[0:1, 1, :].rearrange("p (a b) -> p a b", a=2), AX.X, ALU.max))
            for a in range(2):
                link(v.scalar_tensor_tensor(rt[0:1, 4, 4 * a:4 * a + 4], rt[0:1, 1, 4 * a:4 * a + 4], rt[0:1, 3, a:a + 1],
                                            rt[0:1, 7, 4 * a:4 * a + 4], ALU.is_equal, ALU.mult))
            link(v.tensor_reduce(rt[0:1, 5, 0:2], rt[0:1, 4, :].rearrange("p (a b) -> p a b", a=2), AX.X, ALU.max))
            v.tensor_scalar(chosen[:, :], rt[0:1, 5, 0:2], -1.0, 4.0, ALU.mult, ALU.add).then_inc(r_idx, 1)

            def banks(b, dst):
                s0 = PS[:, b * ACC:b * ACC + 1024].rearrange("p (c n) -> p c n", n=512)[:, :, 0:500]
                return ((dst[:, 0:1000].rearrange("p (c n) -> p c n", n=500), s0),
                        (dst[:, 1000:1250], PS[:, b * ACC + 1024:b * ACC + 1274]))

            for m in range(KD):
                b = m % 2
                dve.wait_ge(zT_act, m + 1)
                tmp = view(PPT + 10000 + b * 5000, F32, N)
                for d_, s_ in banks(b, tmp):
                    v.tensor_scalar(d_, s_, norms[:, 2, m:m + 1], norms[:, 3, m:m + 1], ALU.mult, ALU.add)
                link(v.tensor_copy(xn[0][:, m, :], y32[b]))
                link(v.tensor_copy(xt[0][:, m, :], tmp))
                v.tensor_tensor(xt[1][:, m, :], tmp, xt[0][:, m, :], ALU.subtract)
                v.tensor_tensor(xn[1][:, m, :], y32[b], xn[0][:, m, :], ALU.subtract).then_inc(zT_dve, 1)
            dve.wait_ge(spb_in, 32)
            dve.wait_ge(tmb_in, 16)
            dve.wait_ge(cols_in, 16 * 6)
            v.tensor_scalar(q_b[:, 0, :], sp_b[:, 1, :], 0.125, None, ALU.mult)
            v.tensor_scalar(q_b[:, 1, :], tm_b[:, 1, :], 0.125, None, ALU.mult)
            v.tensor_scalar(q_b[:, 2, :], cr_b[:, 0, :], 0.125, None, ALU.mult).then_inc(qb_ready, 1)

            def token_values(name, row_bias):
                dve.wait_ge(rows_in[name], 16)
                t0 = TBASE[name]
                n0 = ("SPV", "TMV", "CRV").index(name) * NT
                with dve.Fori(0, NT // 2) as ii:
                    for b in range(2):
                        i = ii * 2 + b
                        dve.wait_ge(accT_done, i + (t0 + 1))
                        v.scalar_tensor_tensor(otok[b], PS[0:TP, b * ACC:b * ACC + D], 1.0 / WS, row_bias[:, :],
                                               ALU.mult, ALU.add).then_inc(accT_free, 1)
                        y = otok[b].rearrange("p (h d) -> p h d", d=HD).unsqueeze(1)
                        dve.wait_ge(accT_free, i + (t0 + 1 + 2))
                        v.tensor_scalar(V[:, ds(i, 1), :, 0:HD], y, 1.0, None, ALU.mult).then_inc(v_hi, 1)
                        dve.wait_ge(v_hi, i + (n0 + 1))
                        v.tensor_tensor(V[:, ds(i, 1), :, HD:2 * HD], y, V[:, ds(i, 1), :, 0:HD], ALU.subtract).then_inc(v_split, 1)

            def attention(a):
                S = att[a]

                def maxima(T, h, it):
                    if T >= NT:
                        return
                    dve.wait_ge(S["s_done"], T * H + h + 1 + it * PER2["step"])
                    n_ = TP * key_tiles(a, T)
                    v.tensor_reduce(nmax[:, h % 2:h % 2 + 1], PS[0:TP, (h % 2) * ACC:(h % 2) * ACC + n_], AX.X, ALU.max,
                                    negate=True).then_inc(S["max_done"], 1)

                def transposed(T, h, it, c):
                    if c >= len(chunks(a, T)):
                        return
                    c0, c1 = chunks(a, T)[c]
                    wait_split(dve, a, "lo", T, h, c, it, 0)
                    if c == 0:
                        dve.wait_ge(S["t_full"], t_before(a, T, h, 1) + it * PER2["turn"])
                    else:
                        dve.wait_ge(S["t2_full"], c_before(a, T, h, 2) + 1 + it * PER2["step"])
                    at = T_BANK if c == 0 else third_group(h)
                    v.tensor_copy(probT[:, c0:c1, :], PS[0:TP, at:at + (c1 - c0) * TP].rearrange("p (k n) -> p k n", n=TP)
                                  ).then_inc(S["t_free" if c == 0 else "t2_free"], 1)

                def third_high(T, h, it):
                    if len(chunks(a, T)) < 3:
                        return
                    c0, c1 = chunks(a, T)[2]
                    dve.wait_ge(S["t2_free"], c_before(a, T, h, 2) + 1 + it * PER2["step"])
                    if T * H + h >= 2:
                        dve.wait_ge(S["av_done"], T * H + h - 1 + it * PER2["step"])
                    v.tensor_copy(pT_hi[h % 2][:, c0:c1, :], probT[:, c0:c1, :]).then_inc(S["hi_2"], 1)

                o = PS[0:TP, O_BANK:O_BANK + D].rearrange("p (h d) -> p h d", d=2 * HD)

                def output_hi(T, half, it):
                    heads, n_ = slice(4 * half, 4 * half + 4), 2 * T + half
                    dve.wait_ge(S["av_done"], T * H + 4 * half + 4 + it * PER2["step"])
                    if n_:
                        dve.wait_ge(S["o_ready"], n_ + it * PER2["half"])
                    v.reciprocal(rinv[:, T % 2, heads], rsum[:, T % 2, heads]).then_inc(o_ch, 1)
                    v.tensor_copy(osum, o[:, :, 0:HD]).then_inc(o_ch, 1)

                def output_sum(T, half, it):
                    dve.wait_ge(o_ch, 2 * (2 * a * NT + 2 * T + half + 1) + it * (2 * PER2["half"]))
                    v.tensor_tensor(osum, o[:, :, HD:2 * HD], osum, ALU.add).then_inc(S["o_read"], 1)

                def output_scaled(T, half, it):
                    heads = slice(4 * half, 4 * half + 4)
                    dve.wait_ge(S["o_read"], 2 * T + half + 1 + it * PER2["half"])
                    v.tensor_tensor(otok[T % 2].rearrange("p (h d) -> p h d", d=HD)[:, heads, :], osum,
                                    rinv[:, T % 2, heads].unsqueeze(2).broadcast_to([TP, H // 2, HD]), ALU.mult).then_inc(S["o_ready"], 1)

                def body(T, it):
                    for h in range(H):
                        transposed(T, h, it, 0)
                        if h == 5 or (h == 1 and T >= 1):
                            output_scaled(*((T, 0) if h == 5 else (T - 1, 1)), it)
                        maxima(*((T, h + 2) if h + 2 < H else (T + 1, h + 2 - H)), it)
                        transposed(T, h, it, 2)
                        if h == 4 or (h == 0 and T >= 1):
                            output_hi(*((T, 0) if h == 4 else (T - 1, 1)), it)
                        third_high(T, h, it)
                        if h == 4 or (h == 0 and T >= 1):
                            output_sum(*((T, 0) if h == 4 else (T - 1, 1)), it)

                maxima(0, 0, 0)
                maxima(0, 1, 0)
                attention_tiles(dve, a, body)
                for part in (output_hi, output_sum, output_scaled):
                    part(NT - 1, 1, 0)

            split_features("SPK", None, k_moved, 0, 64)
            keys_moved(dve, 1)
            split_features("SPQ", None, q_moved, 0, 128)
            token_values("SPV", bb[1])
            attention(0)
            split_features("SPO", so)
            split_features("TMK", None, k_moved, 128, 64)
            keys_moved(dve, 2)
            split_features("TMQ", None, q_moved, 256, 128)
            token_values("TMV", bb[0])
            attention(1)
            split_features("TMP", to, add=to)
            split_features("CRQ", None, q_moved, 512, 128)
            queries_moved(dve, 3)
            split_features("CRK", None, k_moved, 256, 64)
            token_values("CRV", bb[1])
            attention(2)
            dve.wait_ge(x0b_ready, 1)
            with dve.Fori(0, NT // 2) as ii:
                for b in range(2):
                    i = ii * 2 + b
                    dve.wait_ge(accT_done, i + (TBASE["CRO"] + 1))
                    v.scalar_tensor_tensor(x2[:, ds(i, 1), :], PS[0:TP, b * ACC:b * ACC + D].unsqueeze(1), 1.0 / WS, x2[:, ds(i, 1), :],
                                           ALU.mult, ALU.add).then_inc(accT_free, 1)
            dve.wait_ge(accT_free, TBASE["CRO"] + NT + 2)
            normalised(z2, x2, 5).then_inc(z2_ready, 1)
            for m in range(KD):
                b = m % 2
                dve.wait_ge(zT_act, 4 + m + 1)
                link(v.tensor_copy(h2[0][:, m, :], y32[b]))
                v.tensor_tensor(h2[1][:, m, :], y32[b], h2[0][:, m, :], ALU.subtract).then_inc(zT_dve, 1)
            for j in range(4):
                split_features(f"UP{j}", gT, off=4 * j)
            dve.wait_ge(x1b_ready, 1)
            with dve.Fori(0, NT // 2) as ii:
                for b in range(2):
                    i = ii * 2 + b
                    dve.wait_ge(accT_done, i + (TBASE["DN"] + 1))
                    v.scalar_tensor_tensor(x2[:, ds(i, 1), :], PS[0:TP, b * ACC:b * ACC + D].unsqueeze(1), 1.0 / WS, x2[:, ds(i, 1), :],
                                           ALU.mult, ALU.add).then_inc(accT_free, 1)


def kernel(**inputs):
    import concourse.bacc as bacc
    from concourse.bass_utils import run_bass_kernel_spmd

    a = {k.replace("L0_", ""): np.asarray(v) for k, v in inputs.items()}

    def w(m):
        m = np.swapaxes(m, -1, -2)
        m = m.reshape(*m.shape[:-2], m.shape[-2] // 128, 128, m.shape[-1])
        return np.swapaxes(m, -3, -2)

    def cols(m):
        return np.swapaxes(m.reshape(*m.shape[:-1], m.shape[-1] // 128, 128), -1, -2)

    s_in, s_b = a["ffn_sp_in_w"].reshape(4, 3, D, D), a["ffn_sp_in_b"].reshape(4, 3, D)
    c_in, c_b = a["ffn_cross_in_w"].reshape(3, D, D), a["ffn_cross_in_b"].reshape(3, D)
    laid = {
        "x": a["x"],
        "src_t": a["src"].reshape(EC, TP).T, "dst_t": a["dst"].reshape(EC, TP).T,
        "dst_g": a["dst"].reshape(NG, GC * TP),
        "attr_t": a["edge_attr_3"].reshape(EC, TP, 3).transpose(1, 2, 0),
        "conf": np.concatenate([a["gnn_conf_w"], a["gnn_conf_b"][None]], axis=1),
        "lin_w": w(a["gnn_lin_w"]), "lin_b": a["gnn_lin_b"][None],
        "norms": np.stack([a[f"ffn_norm_{n}"] for n in ("s_w", "s_b", "t_w", "t_b", "mlp_w", "mlp_b")])
        .reshape(6, KD, 128).transpose(2, 0, 1),
        "r_w1": w(a["ffn_router_w1"]), "r_b1": a["ffn_router_b1"][:, None],
        "r_w2": a["ffn_router_w2"].T, "r_b2": a["ffn_router_b2"][None],
        "sp_w": w(s_in), "sp_kqb": cols(s_b[:, [1, 0]]).transpose(0, 2, 1, 3), "sp_vb": s_b[:, 2],
        "sp_ow": w(a["ffn_sp_out_w"]), "sp_ob": cols(a["ffn_sp_out_b"]),
        "tm_w": w(np.stack([a[f"ffn_t{n}_w"] for n in "qkvp"], axis=1)),
        "tm_kqpb": cols(np.stack([a[f"ffn_t{n}_b"] for n in "kqp"], axis=1)).transpose(0, 2, 1, 3), "tm_vb": a["ffn_tv_b"],
        "cr_w": w(c_in), "cr_qkb": cols(c_b[:2]).transpose(1, 0, 2), "cr_vb": c_b[2:],
        "cr_ow": w(a["ffn_cross_out_w"]), "cr_ob": a["ffn_cross_out_b"][None],
        "up_w": w(a["ffn_mlp_w1"].reshape(4, D, D)), "up_b": cols(a["ffn_mlp_b1"]),
        "dn_w": w(a["ffn_mlp_w2"].reshape(D, 4, D).transpose(1, 0, 2)), "dn_b": a["ffn_mlp_b2"][None],
    }
    nc = bacc.Bacc("TRN2", target_bir_lowering=False, num_devices=1, dynamic_dma_scratch_size=1024)
    arrays, handles = {}, {}
    for name, v in laid.items():
        v = np.ascontiguousarray(v)
        arrays[f"in_{name}"] = v
        handles[name] = nc.dram_tensor(f"in_{name}", v.shape, mybir.dt.from_np(v.dtype), kind="ExternalInput").ap()
    out = nc.dram_tensor("out", (N, D), F32, kind="ExternalOutput").ap()
    build(nc, handles, out)
    return run_bass_kernel_spmd(nc, [arrays], core_ids=[0]).results[0]["out"]
```

```python
from contextlib import ExitStack

import concourse.bass as bass
import numpy as np
from concourse import mybir

F32, F16, BF16, I32 = mybir.dt.float32, mybir.dt.float16, mybir.dt.bfloat16, mybir.dt.int32
ACT, ALU, AX = mybir.ActivationFunctionType, mybir.AluOpType, mybir.AxisListType

N, D, E = 1250, 512, 41250
TP = 125
NT = N // TP
EC = E // TP
KD = D // 128
H, HD = 8, 64
DFF = 4 * D
GC = 5
NG = EC // GC
WIN = 50
NW = N // WIN
WU = 8
KW = WIN * NT
PACK = 128
LS = 2048.0
HOT_PARTS = 5
WS = 64.0
ES = 1024.0
EPS = 1e-5
MASKED = -3.0e38
Z2_DVE = 6
SPLITS = [(0, 512), (512, 1024), (1024, N)]
ACC = 1536
AV_FIRST = 3
T_BANK, O_BANK = 3072, 3584
LIN, SPK, SPQ, SPV, SPO, TMK, TMQ, TMV, TMP, CRQ, CRK, CRV, CRO, UP0, DN0 = *range(14), 17
UNITS, SLOTS = 21, 4


def build(nc, A, out):
    ctx = ExitStack()
    with ctx:
        def sb(name, shape, dt):
            return ctx.enter_context(nc.sbuf_tensor(name, shape, dt))

        def sem(name):
            return ctx.enter_context(nc.semaphore(name))

        UNIT = KD * D * 4
        ROW = NT * D * 4
        R1, R2, R3 = 0, ROW, 2 * ROW
        QKV = 3 * ROW
        PPT = QKV + 4 * ROW
        OREG = PPT + ROW + 4608
        WST = OREG + 9216
        WSL = WST + UNIT
        arena = sb("arena", [128, (WSL + SLOTS * UNIT) // 4], F32)

        def view(at, dt, *dims, parts=128):
            size = 2 if dt in (F16, BF16) else 4
            n = int(np.prod(dims)) * size
            n4 = (n + 3) // 4
            v = arena[0:parts, at // 4:at // 4 + n4]
            if dt != F32:
                v = v.bitcast(dt)
            v = v[:, 0:int(np.prod(dims))]
            if len(dims) == 2:
                v = v.rearrange("p (a b) -> p a b", b=dims[1])
            if len(dims) == 3:
                v = v.rearrange("p (a b c) -> p a b c", b=dims[1], c=dims[2])
            return v

        HALF = ROW // 2

        def pair(at):
            return view(at, F16, KD, N), view(at + HALF, F16, KD, N)

        adj = [view(R1 + i * NT * N * 2, F16, NT, N, parts=TP) for i in range(2)]
        src_i = view(R1, I32, EC, parts=TP)
        dst_i = view(R1 + 1400, I32, EC, parts=TP)
        attr = view(R1 + 2800, F32, 3, EC, parts=TP)
        dst_g = view(R1 + 7000, I32, GC * TP, parts=NG)
        hi_hot = view(R1 + 9600, F16, EC, NT, parts=TP)
        ew = view(R1 + 16400, F32, EC, parts=TP)
        win_v = view(R1 + 18000, F32, 2 * NW, parts=NG)
        win_t = view(R1 + 20000, F32, NW, parts=NG)
        src_f = view(R1 + 22000, F32, EC, parts=TP)
        w16 = view(R1 + 24000, F16, EC, parts=TP)
        lo_hot = view(QKV, F16, EC, TP, parts=TP)
        EA = PPT + 2560
        src_hi = view(EA, F32, EC, parts=TP)
        src_lo = view(EA + 1400, F32, EC, parts=TP)
        krel = [view(EA + 2800, F32, EC, parts=TP), view(EA + 4200, F32, EC, parts=TP)]
        w_hi = view(EA + 5600, F32, EC, parts=TP)
        w_lo = view(EA + 7000, F32, EC, parts=TP)
        w_ratio = view(EA + 8400, F32, EC, parts=TP)
        key_hot = view(PPT + 14100, F16, GC, KW, parts=TP)
        low_part = [view(PPT + 20400 + 2048 * i, F32, KW, parts=TP) for i in range(2)]
        low_hot = view(PPT + 19120, F16, GC, TP, parts=TP)
        xs = view(WSL + UNIT, F32, NT, D, parts=TP)
        xs_split = [view(QKV + 3 * ROW + i * NT * D * 2, F16, NT, D, parts=TP) for i in range(2)]
        high_part = [view(OREG + 2048 * i, F32, KW, parts=TP) for i in range(2)]
        win_sum = view(OREG + 4096, F32, KW, parts=TP)
        agg = pair(QKV)
        x1 = view(QKV + ROW, F32, NT, D, parts=TP)
        xb = view(QKV + 2 * ROW, F32, NT, D, parts=TP)
        x0 = xb
        z0 = view(QKV + 3 * ROW, F32, NT, D, parts=TP)
        xn, xt = pair(R1), pair(R3)
        at_, so, to = pair(R1), pair(R2), pair(R3)
        QA = view(QKV, F16, H, N)
        QB = view(QKV + ROW, F16, H, N)
        K2 = view(QKV + 2 * ROW, F16, H, N)
        V = view(QKV + 3 * ROW, F16, NT, H, 2 * HD, parts=TP)
        prob = [view(PPT + i * 5000, F32, N, parts=TP) for i in range(2)]
        probT = view(PPT + 10000, F32, NT, TP, parts=TP)
        probT_odd = view(OREG + 7168, F32, 4, TP, parts=TP)
        pT_hi = [view(PPT + 15000 + i * 2500, F16, NT, TP, parts=TP) for i in range(2)]
        pT_lo = [view(PPT + 20000 + i * 2500, F16, NT, TP, parts=TP) for i in range(2)]
        y32 = [view(PPT + i * 5000, F32, N) for i in range(2)]
        xt32 = [view(QKV + m * 5000, F32, N) for m in range(KD)]
        part_hi = [view(PPT + 10000 + i * 2500, F16, N) for i in range(2)]
        part_lo = [view(PPT + 15000 + i * 2500, F16, N) for i in range(2)]
        otok = [view(OREG + i * 2048, F32, D, parts=TP) for i in range(2)]
        osum = view(OREG + 4096, F32, H // 2, HD, parts=TP)
        oT = view(OREG + 5120, F32, KD, TP)
        x2 = view(R2, F32, NT, D, parts=TP)
        z2 = view(R3, F32, NT, D, parts=TP)
        x1b = z2
        h2 = pair(R1)
        gT = (view(QKV, F16, DFF // 128, N), view(QKV + 2 * ROW, F16, DFF // 128, N))
        w_in = view(WST, F32, KD, D)
        WH = [view(WSL + i * UNIT, F16, KD, D) for i in range(SLOTS)]
        WL = [view(WSL + i * UNIT + UNIT // 2, F16, KD, D) for i in range(SLOTS)]


        def split_weights(unit):
            if unit == UNITS - 1:
                return view(PPT + 10000, F16, KD, D), view(PPT + 10000 + UNIT // 2, F16, KD, D)
            return WH[unit % SLOTS], WL[unit % SLOTS]

        ident = sb("ident", [128, 128], F32)
        ident_b = sb("ident_b", [TP, TP], BF16)
        mask = sb("mask", [TP, TP], BF16)
        iota = sb("iota", [TP, KW], F16)
        zeros = sb("zeros", [TP, TP], F16)
        bb = [sb(f"bias_rows{i}", [TP, D], F32) for i in range(2)]
        win25 = view(EA + 11400, F32, NW, parts=NG)
        group1 = sb("group1", [NG, 1], F32)
        groupr = sb("groupr", [NG, 1], F32)
        dmm = sb("dmm", [NG, 2], F32)
        rmax = sb("rmax", [2 * NW, 1], F32)
        rows = view(EA + 9800, F32, 4, 64, parts=1)
        visits = view(EA + 11000, I32, NW + 1, parts=1)
        confw = sb("confw", [TP, 4], F32)
        stat = sb("stat", [TP, NT, 6], F32)
        mv = sb("mv", [TP, NT, 2], F32)
        rstd = sb("rstd", [TP, NT], F32)
        nmr = sb("nmr", [TP, NT], F32)
        var = sb("var", [TP, NT], F32)
        newton = sb("newton", [TP, NT], F32)
        deg = sb("deg", [TP, NT], F32)
        dis = sb("dis", [TP, NT], F32)
        dis_s = sb("dis_s", [TP, NT], F32)
        ones = sb("ones", [TP, 1], F32)
        kw_col = sb("kw_col", [TP, 1], F32)
        deg3 = view(OREG, F32, 3 * TP, parts=3 * NT)
        norms = sb("norms", [128, 6, KD], F32)
        sp_b = sb("sp_b", [128, 2, KD], F32)
        sp_ob = sb("sp_ob", [128, KD], F32)
        tm_b = sb("tm_b", [128, 3, KD], F32)
        cr_b = sb("cr_b", [128, 2, KD], F32)
        up_b = sb("up_b", [128, 16], F32)
        q_b = sb("q_b", [128, 3, KD], F32)
        rw1 = view(WST, F32, KD, 128)
        rw2 = sb("rw2", [128, 8], F32)
        rb1 = sb("rb1", [128, 1], F32)
        rb2 = sb("rb2", [1, 8], F32)
        pooled = sb("pooled", [128, KD], F32)
        means_row = view(OREG, F32, D, parts=1)
        hid = sb("hid", [128, 1], F32)
        rt = sb("rt", [1, 8, 8], F32)
        chosen = sb("chosen", [1, 2], I32)
        nmax = sb("nmax", [TP, 2], F32)
        rsum = sb("rsum", [TP, 2, H], F32)
        rinv = sb("rinv", [TP, 2, H], F32)
        PS = ctx.enter_context(nc.psum_tensor("PS", [128, 4096], F32))

        x1_d = nc.dram_tensor("x1_spill", (NT, TP, D), F32, kind="Internal").ap()
        x0_d = nc.dram_tensor("x0_spill", (NT, TP, D), F32, kind="Internal").ap()

        edges_in, conf_in, cols_in, x_in, xr_in = (sem(s) for s in ("edges_in", "conf_in", "cols_in", "x_in", "xr_in"))
        linb_in, rw_in = sem("linb_in"), sem("rw_in")
        consts = sem("consts")
        pool_ch = sem("pool_ch")
        dve_ch = sem("dve_ch")
        act_ch = sem("act_ch")
        logit_ready, ew_ready = sem("logit_ready"), sem("ew_ready")
        hi_ready = sem("hi_ready")
        lo_ready, lo_diff = sem("lo_ready"), sem("lo_diff")
        bounds_ready, boundsT, rmax_ready, rows_done, visits_ready = (
            sem(s) for s in ("bounds_ready", "boundsT", "rmax_ready", "rows_done", "visits_ready"))
        deg_done, deg3_ready, xs_scale, xs_ready = (
            sem(s) for s in ("deg_done", "deg3_ready", "xs_scale", "xs_ready"))
        krel_ready, win_free, win_done, win_high, win_summed, low_added = (
            sem(s) for s in ("krel_ready", "win_free", "win_done", "win_high", "win_summed", "low_added"))
        xs_halves, last_added = sem("xs_halves"), sem("last_added")
        hot_free = [sem(f"hot_free{g}") for g in range(GC)]
        key_made = [sem(f"key_made{g}") for g in range(GC)]
        low_made = [sem(f"low_made{g}") for g in range(GC)]
        w_loaded, w_taken, w_split = sem("w_loaded"), sem("w_taken"), sem("w_split")
        accF_done, accF_read = sem("accF_done"), sem("accF_read")
        v_hi = sem("v_hi")
        x1_ready, nmr_ready, z2_act, xt_low, xt_high = (
            sem(s) for s in ("x1_ready", "nmr_ready", "z2_act", "xt_low", "xt_high"))
        accT_done, accT_free = sem("accT_done"), sem("accT_free")
        y_split, hi_done, res_done, o_ch = sem("y_split"), sem("hi_done"), sem("res_done"), sem("o_ch")
        k_moved, q_moved = [sem(f"k_moved{b}") for b in range(2)], [sem(f"q_moved{b}") for b in range(2)]
        xb_ready, var_ready, std_ready = sem("xb_ready"), sem("var_ready"), sem("std_ready")
        x0_ready, z0_ready, spilled, x0_in, x0b_ready = (
            sem(s) for s in ("x0_ready", "z0_ready", "spilled", "x0_in", "x0b_ready"))
        r_pool, r_row, r_poolc, r_hid, r_gelu, r_log, r_max, r_exp, r_idx = (
            sem(s) for s in ("r_pool", "r_row", "r_poolc", "r_hid", "r_gelu", "r_log", "r_max", "r_exp", "r_idx"))
        zT_done, zT_act, zT_dve, spb_in, tmb_in = (sem(s) for s in ("zT_done", "zT_act", "zT_dve", "spb_in", "tmb_in"))
        rows_in = {s: sem(f"rows_{s}_in") for s in ("SPV", "TMV", "CRV", "CRO", "DN")}
        qb_ready = sem("qb_ready")
        z2_ready, x1_in, x1b_ready, out_done = (sem(s) for s in ("z2_ready", "x1_in", "x1b_ready", "out_done"))
        att = [{s: sem(f"{a}_{s}") for s in ("s_done", "max_done", "exp_done", "t_full", "t_free", "t2_full", "t2_free", "av_done",
                                             "o_read", "o_ready", "oT_hi", "oT_lo", "hi_0", "hi_1", "hi_2",
                                             "lo_0", "lo_1", "lo_2")} for a in ("sp", "tm", "cr")]

        block = ctx.enter_context(nc.Block())
        f_tiles, t_tiles = [0], [0]

        FBASE, TBASE = {}, {}
        for name, n in (("agg", 4), ("SPK", 4), ("SPQ", 4), ("SPO", 4), ("TMK", 4), ("TMQ", 4), ("TMP", 4),
                        ("CRQ", 4), ("CRK", 4), ("UP0", 4), ("UP1", 4), ("UP2", 4), ("UP3", 4)):
            FBASE[name] = f_tiles[0]
            f_tiles[0] += n
        for name in ("LIN", "SPV", "TMV", "CRV", "CRO", "DN"):
            TBASE[name] = t_tiles[0]
            t_tiles[0] += NT

        def key_tiles(a, T):
            return T + 1 if a == 1 else NT

        def chunks(a, T):
            n = key_tiles(a, T)
            return [(c, min(c + 4, n)) for c in range(0, n, 4)]

        def t_before(a, T, h, c=0):
            per = [min(len(chunks(a, t)), 2) for t in range(T + 1)]
            turns = H * sum(per[:T]) + h * per[T] + min(c, per[T])
            return turns + (max(T - 1, 0) + (1 if T >= 1 and h > 2 else 0))

        def transposed_group(a, T, h, c):
            c0, c1 = chunks(a, T)[c]
            return probT_odd[:, 0:c1, :] if c == 0 and h % 2 else probT[:, c0:c1, :]

        def tile_columns(T, it):
            return slice(T * TP, (T + 1) * TP) if isinstance(it, int) else bass.ds(it * (2 * TP) + T * TP, TP)

        def third_group(h):
            return ((h + 1) % 2) * ACC + N

        def c_before(a, T, h, c):
            return (T - (4 * c if a == 1 else 0)) * H + h

        def wait_split(engine, a, which, T, h, c, it, done):
            n = c_before(a, T, h, c) + done
            if n > 0:
                engine.wait_ge(att[a][f"{which}_{c}"], n + it * PER2["step"])

        def attention_tiles(engine, a, body):
            if a == 1:
                for T in range(NT):
                    body(T, 0)
                return
            body(0, 0)
            body(1, 0)
            with engine.Fori(0, 3) as it:
                body(2, it)
                body(3, it)
            body(8, 0)
            body(9, 0)

        def windows(engine, body, before_window=None, after_window=None):
            def window(w, p, packed):
                at = slice(1, 2) if isinstance(w, int) else bass.ds(w + 1, 1)
                after = engine.value_load(visits[0:1, at], min_val=0, max_val=NW * NG * PACK)
                if before_window:
                    before_window(w, p)
                with engine.Fori(packed // PACK, after // PACK) as visit:
                    group = nc.s_assert_within(visit - packed // PACK + packed % PACK, 0, NG - 1,
                                               skip_runtime_bounds_check_because="the table bounds it")
                    body(p, visit, group)
                if after_window:
                    after_window(w, p)
                return after

            window(0, 0, engine.value_load(visits[0:1, 0:1], min_val=0, max_val=NW * NG * PACK))
            with engine.Fori(0, NW // WU) as ww:
                packed = engine.value_load(visits[0:1, bass.ds(ww * WU + 1, 1)], min_val=0, max_val=NW * NG * PACK)
                for j in range(WU):
                    packed = window(ww * WU + (j + 1), (j + 1) % 2, packed)

        def part_chunks(part):
            return slice(part * (EC // HOT_PARTS), (part + 1) * (EC // HOT_PARTS))

        def source_hots(vector, part):
            n_, c = EC // HOT_PARTS, part_chunks(part)
            vector.tensor_tensor(lo_hot[:, c, :], src_lo[:, c].unsqueeze(2).broadcast_to([TP, n_, TP]),
                                 iota[:, 0:TP].unsqueeze(1).broadcast_to([TP, n_, TP]), ALU.is_equal).then_inc(lo_ready, 1)

        def window_adj(w, half):
            at = slice(WIN * w, WIN * (w + 1)) if isinstance(w, int) else bass.ds(w * WIN, WIN)
            return adj[half][:, :, at]

        def keys_moved(engine, count):
            for b in range(2):
                engine.wait_ge(k_moved[b], 64 + 128 * count)

        def queries_moved(engine, count):
            for b in range(2):
                engine.wait_ge(q_moved[b], 128 + 256 * count)

        def heads_moved(engine, count):
            keys_moved(engine, count)
            queries_moved(engine, count)

        PER2 = {"step": 2 * H, "turn": 2 * (H * 2 + 1), "tile": 2, "half": 4}

        @block.sync
        def _(sp):
            sp.dma_start(dst_g, A["dst_g"]).then_inc(edges_in, 16)
            sp.dma_start(src_i, A["src_t"]).then_inc(edges_in, 16)
            sp.dma_start(dst_i, A["dst_t"]).then_inc(edges_in, 16)
            sp.dma_start(attr, A["attr_t"]).then_inc(edges_in, 16)
            sp.dma_start(xs, A["x"].rearrange("(t p) d -> p t d", p=TP)).then_inc(x_in, 16)

            def load(unit, src):
                if unit >= 1:
                    sp.wait_ge(w_taken, unit)
                sp.dma_start(w_in, src).then_inc(w_loaded, 16)

            load(LIN, A["lin_w"])
            sp.wait_ge(win_done, NW)
            sp.dma_start(xb, A["x"].rearrange("(t p) d -> p t d", p=TP)).then_inc(xr_in, 16)
            sp.wait_ge(w_taken, 1)
            sp.dma_start(rw1, A["r_w1"]).then_inc(rw_in, 16)
            sp.wait_ge(x1_ready, 1)
            sp.dma_start(x1_d.rearrange("t p d -> p t d"), x1).then_inc(spilled, 16)
            sp.wait_ge(x0_ready, NT)
            sp.dma_start(x0_d.rearrange("t p d -> p t d"), x0).then_inc(spilled, 16)
            sp.wait_ge(r_idx, 1)
            si = sp.value_load(chosen[0:1, 0:1], min_val=0, max_val=3)
            ti = sp.value_load(chosen[0:1, 1:2], min_val=0, max_val=3)
            ds = bass.ds

            sp.wait_ge(r_hid, 1)
            load(SPK, A["sp_w"][ds(si, 1), 1].rearrange("a p k o -> p (a k) o"))
            sp.dma_start(sp_b[:, :, :], A["sp_kqb"][ds(si, 1)].rearrange("a p u k -> p (a u) k")).then_inc(spb_in, 16)
            sp.dma_start(sp_ob[:, :], A["sp_ob"][ds(si, 1)].rearrange("a p k -> p (a k)")).then_inc(spb_in, 16)
            sp.dma_start(bb[1][:, :], A["sp_vb"][ds(si, 1), :].broadcast_to([TP, D])).then_inc(rows_in["SPV"], 16)
            sp.dma_start(tm_b[:, :, :], A["tm_kqpb"][ds(ti, 1)].rearrange("a p u k -> p (a u) k")).then_inc(tmb_in, 16)
            load(SPQ, A["sp_w"][ds(si, 1), 0].rearrange("a p k o -> p (a k) o"))
            load(SPV, A["sp_w"][ds(si, 1), 2].rearrange("a p k o -> p (a k) o"))
            sp.dma_start(bb[0][:, :], A["tm_vb"][ds(ti, 1), :].broadcast_to([TP, D])).then_inc(rows_in["TMV"], 16)

            def move_heads(fbase, is_q):
                with sp.Fori(0, 2) as mm:
                    for b in range(2):
                        m = mm * 2 + b
                        sp.wait_ge(y_split, m + (fbase + 1 + 2))
                        hi, lo = part_hi[b], part_lo[b]
                        for half, h in ((slice(0, 64), m * 2), (slice(64, 128), m * 2 + 1)):
                            if is_q:
                                for to_ in (slice(0, 64), slice(64, 128)):
                                    sp.dma_start(QA[to_, ds(h, 1), :], hi[half, :]).then_inc(q_moved[b], 16)
                                    sp.dma_start(QB[to_, ds(h, 1), :], lo[half, :]).then_inc(q_moved[b], 16)
                            else:
                                other = slice(64, 128) if half.start == 0 else slice(0, 64)
                                sp.dma_start(K2[half, ds(h, 1), :], hi[half, :]).then_inc(k_moved[b], 16)
                                sp.dma_start(K2[other, ds(h, 1), :], lo[half, :]).then_inc(k_moved[b], 16)

            for b in range(2):
                sp.sem_inc(k_moved[b], 64)
                sp.sem_inc(q_moved[b], 128)
            sp.wait_ge(spilled, 32)
            sp.wait_ge(zT_done, 4)
            move_heads(FBASE["SPK"], False)
            load(SPO, A["sp_ow"][ds(si, 1)].rearrange("a p k o -> p (a k) o"))
            sp.wait_ge(xt_low, KD)
            move_heads(FBASE["SPQ"], True)
            load(TMK, A["tm_w"][ds(ti, 1), 1].rearrange("a p k o -> p (a k) o"))
            load(TMQ, A["tm_w"][ds(ti, 1), 0].rearrange("a p k o -> p (a k) o"))
            sp.wait_ge(accT_free, TBASE["TMV"] + 2)
            sp.dma_start(bb[1][:, :], A["cr_vb"].broadcast_to([TP, D])).then_inc(rows_in["CRV"], 16)
            load(TMV, A["tm_w"][ds(ti, 1), 2].rearrange("a p k o -> p (a k) o"))
            load(TMP, A["tm_w"][ds(ti, 1), 3].rearrange("a p k o -> p (a k) o"))
            move_heads(FBASE["TMK"], False)
            load(CRQ, A["cr_w"][0])
            move_heads(FBASE["TMQ"], True)
            sp.wait_ge(accT_free, TBASE["CRV"] + 2)
            sp.dma_start(bb[0][:, :], A["cr_ob"].broadcast_to([TP, D])).then_inc(rows_in["CRO"], 16)
            load(CRK, A["cr_w"][1])
            load(CRV, A["cr_w"][2])
            move_heads(FBASE["CRQ"], True)
            sp.dma_start(x2, x0_d.rearrange("t p d -> p t d")).then_inc(x0_in, 16)
            move_heads(FBASE["CRK"], False)
            load(CRO, A["cr_ow"])
            sp.wait_ge(accT_free, TBASE["CRO"] + 2)
            sp.dma_start(bb[1][:, :], A["dn_b"].broadcast_to([TP, D])).then_inc(rows_in["DN"], 16)
            for j in range(4):
                load(UP0 + j, A["up_w"][j])
            sp.wait_ge(zT_done, 8)
            sp.dma_start(x1b, x1_d.rearrange("t p d -> p t d")).then_inc(x1_in, 16)
            for j in range(4):
                load(DN0 + j, A["dn_w"][j])
            with sp.Fori(0, NT) as i:
                sp.wait_ge(accT_free, i + (TBASE["DN"] + 3))
                sp.dma_start(out[ds(i * TP, TP), :], x2[:, ds(i, 1), :].rearrange("p a d -> p (a d)")).then_inc(out_done, 16)
            sp.wait_ge(out_done, 16 * NT)

        @block.gpsimd
        def _(pool):
            g = nc.gpsimd
            ds = bass.ds
            n = [0]

            def link(ins):
                n[0] += 1
                ins.then_inc(pool_ch, 1)
                pool.wait_ge(pool_ch, n[0])

            exact = dict(allow_small_or_imprecise_dtypes=True)
            link(g.iota(iota[:, :], [[1, KW]], base=0, channel_multiplier=0, **exact))
            link(g.iota(win25[:, :], [[WIN, NW]], base=0, channel_multiplier=0, **exact))
            link(g.iota(group1[:, :], [[0, 1]], base=1, channel_multiplier=1, **exact))
            link(g.iota(groupr[:, :], [[0, 1]], base=NG, channel_multiplier=-1, **exact))
            link(g.memset(zeros[:, :], 0.0))
            link(g.memset(ident[:, :], 0.0))
            link(g.affine_select(out=ident[:, :], in_=ident[:, :], compare_op=ALU.not_equal, fill=1.0, base=0,
                                 pattern=[[-1, 128]], channel_multiplier=1))
            link(g.memset(ident_b[:, :], 0.0))
            link(g.affine_select(out=ident_b[:, :], in_=ident_b[:, :], compare_op=ALU.not_equal, fill=1.0, base=0,
                                 pattern=[[-1, TP]], channel_multiplier=1))
            link(g.memset(mask[:, :], 0.0))
            link(g.affine_select(out=mask[:, :], in_=mask[:, :], compare_op=ALU.is_ge, fill=MASKED, base=0,
                                 pattern=[[-1, TP]], channel_multiplier=1))
            link(g.iota(rt[0:1, 7, :], [[0, 2], [-1, 4]], base=4, channel_multiplier=0, **exact))
            link(g.memset(kw_col[:, :], float(KW)))
            g.memset(ones[:, :], 1.0).then_inc(consts, 1)

            def split(unit):
                hi, lo = split_weights(unit)
                pool.wait_ge(w_loaded, 16 * (unit + 1))
                link(g.tensor_scalar(w_in, w_in, WS, 1.0, ALU.mult, ALU.mult))
                link(g.tensor_scalar(hi, w_in, 1.0, 1.0, ALU.mult, ALU.mult))
                link(g.tensor_tensor(lo, w_in, hi, ALU.subtract))
                pool.sem_inc(w_taken, 1)
                pool.sem_inc(w_split, 1)

            pool.wait_ge(xs_scale, 1)
            per = NT * WU // NW

            pool.sem_inc(low_added, 2)

            def next_keys(w, p):
                pool.wait_ge(krel_ready, w + 1)
                g.tensor_tensor(krel[1 - p], krel[p], kw_col[:, 0:1].broadcast_to([TP, EC]), ALU.subtract).then_inc(krel_ready, 1)

            def add_low(w, p):
                pool.wait_ge(win_high, w + 1)
                pool.wait_ge(win_free, w + 3)
                a, b = high_part[p], low_part[p]
                g.tensor_tensor(win_sum, a, b, ALU.add).then_inc(win_summed, 1)
                parts = [x.rearrange("p (a d) -> p a d", a=NT) for x in (a, b, win_sum)]
                pool.wait_ge(win_summed, w * 2 + 1)
                g.tensor_tensor(window_adj(w, 0), parts[0], parts[1], ALU.add).then_inc(win_summed, 1)
                pool.wait_ge(win_summed, w * 2 + 2)
                g.tensor_tensor(window_adj(w, 1), parts[2], window_adj(w, 0), ALU.subtract).then_inc(low_added, 1)
                pool.wait_ge(low_added, w + 3)

            def scale_xs(tile, col, k, done):
                by = (rstd, nmr)[k][:, col].unsqueeze(2).broadcast_to([TP, 1, D])
                g.tensor_tensor(xs[:, tile, :], xs[:, tile, :], by, (ALU.mult, ALU.add)[k]).then_inc(xs_ready, 1)
                pool.wait_ge(xs_ready, done)

            next_keys(0, 0)
            extra = NT - NW // WU * per
            for t in range(extra):
                for k in range(2):
                    at = slice(NT - extra + t, NT - extra + t + 1)
                    scale_xs(at, at, k, 2 * t + k + 1)
            with pool.Fori(0, NW // WU) as ww:
                for j in range(WU):
                    w, p = ww * WU + (j + 1), (j + 1) % 2
                    pool.wait_ge(win_done, w)
                    next_keys(w, p)
                    if j < 2 * per:
                        at = ds(ww * per + j // 2, 1)
                        scale_xs(at, at, j % 2, (ww * per + j // 2) * 2 + (j % 2 + 1 + 2 * extra))
                    add_low(ww * WU + j, 1 - p)

            def attention(a):
                S = att[a]

                def output(T, it):
                    pool.wait_ge(S["oT_hi"], T + it * PER2["tile"])
                    cols = tile_columns(T - 1, it)
                    g.tensor_tensor(at_[1][:, :, cols], oT, at_[0][:, :, cols], ALU.subtract).then_inc(S["oT_lo"], 1)

                def body(T, it):
                    for h in range(H):
                        if h == 3 and T >= 1:
                            output(T, it)
                        for c, (c0, c1) in enumerate(chunks(a, T)):
                            wait_split(pool, a, "hi", T, h, c, it, 1)
                            if c == 0 and T * H + h >= 2:
                                pool.wait_ge(S["av_done"], T * H + h - 1 + it * PER2["step"])
                            g.tensor_tensor(pT_lo[h % 2][:, c0:c1, :], transposed_group(a, T, h, c), pT_hi[h % 2][:, c0:c1, :],
                                            ALU.subtract).then_inc(S[f"lo_{c}"], 1)

                attention_tiles(pool, a, body)
                output(NT, 0)

            split(LIN)
            pool.wait_ge(xr_in, 16)
            pool.wait_ge(linb_in, 16)
            for t in range(NT):
                last = g.tensor_tensor(xb[:, t, :], xb[:, t, :], bb[0][:, :], ALU.add)
            link(last)
            pool.sem_inc(xb_ready, 1)
            pool.wait_ge(accF_done, FBASE["SPK"])
            split(SPK)
            for m in range(KD):
                pool.wait_ge(xt_high, m + 1)
                g.tensor_tensor(xt[1][:, m, :], xt32[m], xt[0][:, m, :], ALU.subtract).then_inc(xt_low, 1)
            split(SPQ)
            split(SPV)
            pool.wait_ge(accT_done, TBASE["SPV"])
            split(SPO)
            attention(0)
            pool.wait_ge(accF_done, FBASE["SPK"] + 4)
            split(TMK)
            pool.wait_ge(accF_done, FBASE["SPQ"] + 4)
            split(TMQ)
            pool.wait_ge(accT_done, TBASE["SPV"] + NT)
            split(TMV)
            pool.wait_ge(accF_done, FBASE["SPO"] + 4)
            split(TMP)
            attention(1)
            pool.wait_ge(accF_done, FBASE["TMK"] + 4)
            split(CRQ)
            pool.wait_ge(accF_done, FBASE["TMQ"] + 4)
            split(CRK)
            pool.wait_ge(accT_done, TBASE["TMV"] + NT)
            split(CRV)
            pool.wait_ge(accF_done, FBASE["TMP"] + 4)
            split(CRO)
            pool.wait_ge(x0_in, 16)
            pool.wait_ge(rows_in["CRO"], 16)
            for t in range(NT):
                last = g.tensor_tensor(x2[:, t, :], x2[:, t, :], bb[0][:, :], ALU.add)
            link(last)
            pool.sem_inc(x0b_ready, 1)
            attention(2)
            pool.wait_ge(accF_done, FBASE["CRQ"] + 4)
            split(UP0)
            pool.wait_ge(accF_done, FBASE["CRK"] + 4)
            split(UP0 + 1)
            pool.wait_ge(accT_done, TBASE["CRV"] + NT)
            split(UP0 + 2)
            pool.wait_ge(accT_done, TBASE["CRO"] + NT)
            split(UP0 + 3)
            pool.wait_ge(x1_in, 16)
            pool.wait_ge(rows_in["DN"], 16)
            for t in range(NT):
                link(g.tensor_tensor(x1b[:, t, :], x1b[:, t, :], bb[1][:, :], ALU.add))
                last = g.tensor_tensor(x2[:, t, :], x2[:, t, :], x1b[:, t, :], ALU.add)
            link(last)
            pool.sem_inc(x1b_ready, 1)
            for j in range(4):
                if j < 3:
                    pool.wait_ge(accF_done, FBASE[f"UP{j}"] + 4)
                split(DN0 + j)

        @block.tensor
        def _(pe):
            mm_ = nc.tensor.matmul
            ds = bass.ds
            pe.wait_ge(consts, 1)
            pe.wait_ge(bounds_ready, 1)
            nc.tensor.transpose(PS[0:2 * NW, 0:NG], win_v, ident[0:NG, 0:NG]).then_inc(boundsT, 1)
            pe.wait_ge(rmax_ready, 1)
            mm_(PS[0:1, 512:512 + 2 * NW], rmax[:, :], ident[0:2 * NW, 0:2 * NW], start=True, stop=True).then_inc(rows_done, 1)

            pe.wait_ge(hi_ready, 1)
            DEG = PS[0:3 * NT, 1024:1024 + 3 * TP]
            mm_(DEG, zeros[:, 0:3 * NT], iota[:, 0:1].broadcast_to([TP, 3 * TP]), start=True, stop=False)
            for made, part in enumerate((0, 1, 3, 2, 4)):
                pe.wait_ge(lo_ready, made + 1)
                with pe.Fori(2 * part, 2 * part + 2) as j:
                    for c in range(0, EC // HOT_PARTS // 2, 3):
                        at = ds(j * (EC // HOT_PARTS // 2) + c, 3)
                        last = mm_(DEG, hi_hot[:, at, :], lo_hot[:, at, :], start=False, stop=False)
            mm_(DEG, zeros[:, 0:3 * NT], iota[:, 0:1].broadcast_to([TP, 3 * TP]), start=False, stop=True).then_inc(deg_done, 1)
            pe.wait_ge(deg3_ready, 1)
            for c in range(3):
                last = nc.tensor.transpose(PS[0:TP, 1536 + 3 * NT * c:1536 + 3 * NT * (c + 1)], deg3[:, c * TP:(c + 1) * TP],
                                           ident[0:3 * NT, 0:3 * NT])
            last.then_inc(deg_done, 1)

            pe.wait_ge(visits_ready, 1)
            for g in range(GC):
                pe.sem_inc(hot_free[g], 1)
            pe.sem_inc(win_free, 2)

            def window_acc(p, half):
                at = 2048 + 1024 * p + 512 * half
                return PS[0:TP, at:at + KW]

            def open_window(w, p):
                pe.wait_ge(win_free, w + 1)
                for half in range(2):
                    mm_(window_acc(p, half), zeros[:, :], iota[:, :], start=True, stop=False)

            def close_window(w, p):
                for half in range(2):
                    last = mm_(window_acc(p, half), zeros[:, :], iota[:, :], start=False, stop=True)
                last.then_inc(win_done, 1)

            def add_group(p, visit, group):
                for g in range(GC):
                    pe.wait_ge(key_made[g], visit + 1)
                    mm_(window_acc(p, 0), lo_hot[:, ds(group * GC + g, 1), :], key_hot[:, g, :], start=False, stop=False)
                    pe.wait_ge(low_made[g], visit + 1)
                    mm_(window_acc(p, 1), low_hot[:, g, :], key_hot[:, g, :], start=False, stop=False).then_inc(hot_free[g], 1)

            windows(pe, add_group, open_window, close_window)

            pe.wait_ge(low_added, NW - 1 + 2)
            pe.wait_ge(last_added, 1)
            with pe.Fori(0, 2) as mm:
                for b in range(2):
                    m = mm * 2 + b
                    pe.wait_ge(accF_read, m + 1)
                    for k in range(NT):
                        pe.wait_ge(xs_halves, k + 1)
                        for i, (x_, a_) in enumerate(((0, 0), (0, 1), (1, 0))):
                            for s, e in SPLITS:
                                last = mm_(PS[:, b * ACC + s:b * ACC + e], xs_split[x_][:, k, ds(m * 128, 128)], adj[a_][:, k, s:e],
                                           start=(k == 0 and i == 0), stop=(k == NT - 1 and i == 2))
                    last.then_inc(accF_done, 1)

            def feature_product(name, unit, x):
                f = FBASE[name]
                hi, lo = split_weights(unit)
                pe.wait_ge(w_split, unit + 1)
                with pe.Fori(0, 2) as mm:
                    for b in range(2):
                        m = mm * 2 + b
                        pe.wait_ge(accF_read, m + (f + 1))
                        for k in range(KD):
                            for i, (w, v) in enumerate(((hi, x[0]), (hi, x[1]), (lo, x[0]))):
                                for s, e in SPLITS:
                                    last = mm_(PS[:, b * ACC + s:b * ACC + e], w[:, k, ds(m * 128, 128)], v[:, k, s:e],
                                               start=(k == 0 and i == 0), stop=(k == KD - 1 and i == 2))
                        last.then_inc(accF_done, 1)

            def token_product(name, units, x):
                t0 = TBASE[name]
                pe.wait_ge(w_split, units[-1] + 1)
                with pe.Fori(0, NT // 2) as ii:
                    for b in range(2):
                        i = ii * 2 + b
                        pe.wait_ge(accT_free, i + (t0 + 1))
                        for u, unit in enumerate(units):
                            hi, lo = split_weights(unit)
                            for k in range(KD):
                                for j, (v, w) in enumerate(((x[0], hi), (x[0], lo), (x[1], hi))):
                                    last = mm_(PS[0:TP, b * ACC:b * ACC + D], v[:, u * KD + k, ds(i * TP, TP)], w[:, k, :],
                                               start=(u == 0 and k == 0 and j == 0),
                                               stop=(u == len(units) - 1 and k == KD - 1 and j == 2))
                        last.then_inc(accT_done, 1)

            pe.wait_ge(y_split, FBASE["agg"] + 4 + 2)
            pe.wait_ge(accF_read, FBASE["SPK"] + 2)
            token_product("LIN", [LIN], agg)

            for t in range(NT):
                pe.wait_ge(x0_ready, t + 1)
                last = mm_(PS[0:1, O_BANK:O_BANK + D], ones[:, :], x0[:, t, :], start=(t == 0), stop=(t == NT - 1))
            last.then_inc(r_pool, 1)
            pe.wait_ge(r_row, 1)
            for k in range(KD):
                last = mm_(PS[:, T_BANK + k:T_BANK + k + 1], means_row[:, k * 128:(k + 1) * 128], ones[0:1, :], start=True, stop=True)
            last.then_inc(r_pool, 1)
            pe.wait_ge(rw_in, 16)
            pe.wait_ge(r_poolc, 1)
            for k in range(KD):
                last = mm_(PS[:, O_BANK:O_BANK + 1], rw1[:, k, :], pooled[:, k:k + 1], start=(k == 0), stop=(k == KD - 1))
            last.then_inc(r_hid, 1)
            pe.wait_ge(cols_in, 16 * 6)
            pe.wait_ge(r_gelu, 1)
            mm_(PS[0:1, T_BANK:T_BANK + 8], hid[:, :], rw2[:, :], start=True, stop=True).then_inc(r_log, 1)

            def to_features(z, done_before):
                for m in range(KD):
                    if m >= 2:
                        pe.wait_ge(zT_act, done_before + m - 1)
                    for t in range(NT):
                        at0 = (m % 2) * ACC + (t // 4) * 512 + (t % 4) * TP
                        last = nc.tensor.transpose(PS[:, at0:at0 + TP], z[:, t, m * 128:(m + 1) * 128], ident[0:TP, 0:TP])
                    last.then_inc(zT_done, 1)

            pe.wait_ge(z0_ready, 1)
            to_features(z0, 0)

            def attention(a, causal):
                S = att[a]

                def scores(T, h, it, chunk):
                    width = TP * key_tiles(a, T)
                    nch = (width + 511) // 512
                    if chunk >= nch:
                        return
                    b = h % 2
                    s, e = chunk * 512, min(chunk * 512 + 512, width)
                    acc = PS[0:TP, b * ACC + s:b * ACC + e]
                    qs = ds(it * (2 * TP) + T * TP, TP) if not isinstance(it, int) else slice(T * TP, (T + 1) * TP)
                    diag = (max(s, T * TP), min(e, (T + 1) * TP))
                    masked = causal and diag[0] < diag[1]
                    mm_(acc, QA[:, h, qs], K2[:, h, s:e], start=True, stop=False)
                    last = mm_(acc, QB[:, h, qs], K2[:, h, s:e], start=False, stop=not masked)
                    if masked:
                        last = mm_(PS[0:TP, b * ACC + diag[0]:b * ACC + diag[1]], ident_b[:, :],
                                   mask[:, diag[0] - T * TP:diag[1] - T * TP], start=False, stop=True)
                    if chunk == nch - 1:
                        last.then_inc(S["s_done"], 1)

                def transposes(T, h, it, c):
                    cs = chunks(a, T)
                    if c >= len(cs):
                        return
                    turn = t_before(a, T, h, c)
                    if c < 2 and turn:
                        pe.wait_ge(S["t_free"], turn + it * PER2["turn"])
                    for kt in range(*cs[c]):
                        o = (T_BANK if c < 2 else third_group(h)) + (kt - cs[c][0]) * TP
                        last = nc.tensor.transpose(PS[0:TP, o:o + TP], prob[h % 2][:, kt * TP:(kt + 1) * TP], ident[0:TP, 0:TP])
                    last.then_inc(S["t_full" if c < 2 else "t2_full"], 1)

                def values(T, h, it, part):
                    n_ = key_tiles(a, T)
                    if part == 0 and h % 4 == 0 and (T or h):
                        pe.wait_ge(S["o_read"], 2 * T + h // 4 + it * PER2["half"])
                    last = None
                    for kt in (range(min(AV_FIRST, n_)) if part == 0 else range(AV_FIRST, n_)):
                        if kt % 4 == 0:
                            wait_split(pe, a, "hi", T, h, kt // 4, it, 1)
                            wait_split(pe, a, "lo", T, h, kt // 4, it, 1)
                        for half in (pT_hi, pT_lo):
                            last = mm_(PS[0:TP, O_BANK + (h % 4) * 2 * HD:O_BANK + (h % 4 + 1) * 2 * HD], half[h % 2][:, kt, :],
                                       V[:, kt, h, :], start=(kt == 0 and half is pT_hi), stop=(kt == n_ - 1 and half is pT_lo))
                    if last and kt == n_ - 1:
                        last.then_inc(S["av_done"], 1)

                def output(T, it):
                    turn = t_before(a, T, 3, 0) - 1 if T < NT else t_before(a, NT - 1, H - 1, len(chunks(a, NT - 1)))
                    pe.wait_ge(S["t_free"], turn + it * PER2["turn"])
                    pe.wait_ge(S["o_ready"], 2 * T + it * PER2["half"])
                    for k in range(KD):
                        last = nc.tensor.transpose(PS[:, T_BANK + k * TP:T_BANK + (k + 1) * TP],
                                                   otok[(T - 1) % 2][:, k * 128:(k + 1) * 128], ident[0:TP, 0:TP])
                    last.then_inc(S["t_full"], 1)

                def body(T, it):
                    for h in range(H):
                        later = [(T, h + d) if h + d < H else (T + 1, h + d - H) for d in range(4)]
                        before = (T, h - 1) if h else (T - 1, H - 1)
                        transposes(T, h, it, 0)
                        if later[2][0] < NT:
                            scores(*later[2], it, 1)
                            if c_before(a, T, h, 2) > 0:
                                pe.wait_ge(S["t2_free"], c_before(a, T, h, 2) + it * PER2["step"])
                            scores(*later[2], it, 2)
                        if T or h:
                            values(*before, it, 0)
                        transposes(T, h, it, 1)
                        if T or h:
                            values(*before, it, 1)
                        if h == 2 and T >= 1:
                            output(T, it)
                        if later[1][0] < NT:
                            pe.wait_ge(S["exp_done"], T * H + h + 2 + it * PER2["step"])
                        transposes(T, h, it, 2)
                        if later[3][0] < NT:
                            scores(*later[3], it, 0)

                for h in range(2):
                    for c in range(3):
                        scores(0, h, 0, c)
                pe.wait_ge(S["exp_done"], 1)
                scores(0, 2, 0, 0)
                attention_tiles(pe, a, body)
                values(NT - 1, H - 1, 0, 0)
                values(NT - 1, H - 1, 0, 1)
                output(NT, 0)

            def stage_clear(f, t):
                pe.wait_ge(accF_read, f + 2)
                pe.wait_ge(accT_free, t + 2)

            FB, TB = FBASE, TBASE
            pe.wait_ge(y_split, FB["SPK"] + 2)
            pe.wait_ge(zT_act, 4)
            pe.wait_ge(zT_dve, 4)
            feature_product("SPK", SPK, xn)
            feature_product("SPQ", SPQ, xn)
            stage_clear(FB["SPO"], TB["SPV"])
            token_product("SPV", [SPV], xn)
            stage_clear(FB["SPO"], TB["TMV"])
            heads_moved(pe, 1)
            attention(0, False)
            pe.wait_ge(att[0]["oT_lo"], NT)
            feature_product("SPO", SPO, at_)
            pe.wait_ge(xt_low, KD)
            feature_product("TMK", TMK, xt)
            feature_product("TMQ", TMQ, xt)
            stage_clear(FB["TMP"], TB["TMV"])
            token_product("TMV", [TMV], xt)
            stage_clear(FB["TMP"], TB["CRV"])
            heads_moved(pe, 2)
            attention(1, True)
            pe.wait_ge(att[1]["oT_lo"], NT)
            feature_product("TMP", TMP, at_)
            feature_product("CRQ", CRQ, so)
            pe.wait_ge(y_split, FB["TMP"] + 4 + 2)
            feature_product("CRK", CRK, to)
            stage_clear(FB["UP0"], TB["CRV"])
            token_product("CRV", [CRV], to)
            stage_clear(FB["UP0"], TB["CRO"])
            heads_moved(pe, 3)
            attention(2, False)
            pe.wait_ge(att[2]["oT_lo"], NT)
            token_product("CRO", [CRO], at_)
            pe.wait_ge(z2_ready, 1)
            pe.wait_ge(z2_act, 1)
            to_features(z2, 4)
            pe.wait_ge(zT_act, 8)
            pe.wait_ge(zT_dve, 8)
            for j in range(4):
                feature_product(f"UP{j}", UP0 + j, h2)
            pe.wait_ge(y_split, FB["UP3"] + 4 + 2)
            stage_clear(FB["UP3"] + 4, TB["DN"])
            token_product("DN", [DN0 + j for j in range(4)], gT)

        @block.scalar
        def _(act):
            a_ = nc.scalar.activation
            ds = bass.ds
            act.dma_start(confw[:, :], A["conf"].broadcast_to([TP, 4])).then_inc(conf_in, 16)
            act.dma_start(bb[0][:, :], A["lin_b"].broadcast_to([TP, D])).then_inc(linb_in, 16)
            act.dma_start(norms[:, :, :], A["norms"]).then_inc(cols_in, 16)
            act.dma_start(cr_b[:, :, :], A["cr_qkb"]).then_inc(cols_in, 16)
            act.dma_start(up_b[:, :], A["up_b"]).then_inc(cols_in, 16)
            act.dma_start(rw2[:, :], A["r_w2"]).then_inc(cols_in, 16)
            act.dma_start(rb1[:, :], A["r_b1"]).then_inc(cols_in, 16)
            act.dma_start(rb2[:, :], A["r_b2"]).then_inc(cols_in, 16)
            act.wait_ge(conf_in, 16)
            act.wait_ge(logit_ready, 1)
            a_(ew, ew, ACT.Sigmoid, bias=confw[:, 3:4]).then_inc(ew_ready, 1)

            act.wait_ge(krel_ready, 1)
            act.wait_ge(consts, 1)
            first, per_step = 3 * (EC // HOT_PARTS), 12
            with act.Fori(0, (EC - first) // per_step) as j:
                for c in range(per_step):
                    at = ds(j * per_step + (first + c), 1)
                    a_(lo_hot[:, at, :], iota[:, 0:TP].unsqueeze(1), ACT.Identity, scale=-1.0, bias=src_lo[:, at]).then_inc(lo_diff, 1)

            roots = [0]

            def root(dst, src):
                roots[0] += 1
                act.wait_ge(var_ready, roots[0])
                a_(dst, src, ACT.Sqrt).then_inc(std_ready, 1)

            root(rstd[:, :], rstd[:, :])
            root(dis[:, :], dis[:, :])
            act.wait_ge(visits_ready, 1)

            def low_halves(p, visit, group):
                for g in range(GC):
                    act.wait_ge(hot_free[g], visit + 1)
                    c = ds(group * GC + g, 1)
                    a_(low_hot[:, g, :].unsqueeze(1), lo_hot[:, c, :], ACT.Copy, scale=w_ratio[:, c]).then_inc(low_made[g], 1)

            def read_window(w, p):
                act.wait_ge(win_done, w + 1)
                at = 2048 + 1024 * p
                act.wait_ge(low_added, w + 1)
                a_(high_part[p].rearrange("p (a d) -> p d a", a=NT), PS[0:TP, at:at + KW].rearrange("p (d a) -> p d a", a=NT),
                   ACT.Copy, scale=1.0 / ES).then_inc(win_high, 1)
                a_(low_part[p].rearrange("p (a d) -> p d a", a=NT), PS[0:TP, at + 512:at + 512 + KW].rearrange("p (d a) -> p d a", a=NT),
                   ACT.Copy, scale=1.0 / (ES * LS)).then_inc(win_free, 1)

            def read_before(w, p):
                if not isinstance(w, int):
                    read_window(w - 1, 1 - p)

            windows(act, low_halves, None, read_before)
            read_window(NW - 1, (NW - 1) % 2)

            act.sem_inc(accF_read, 2)

            def read_features(name, bias, scale=1.0 / WS, fn=ACT.Identity):
                f = FBASE[name]
                with act.Fori(0, 2) as mm:
                    for b in range(2):
                        m = mm * 2 + b
                        act.wait_ge(accF_done, m + (f + 1))
                        act.wait_ge(y_split, m + (f + 1))
                        extra = {} if bias is None else {"bias": bias[:, ds(m, 1)]}
                        a_(y32[b], PS[:, b * ACC:b * ACC + N], fn, scale=scale, **extra).then_inc(accF_read, 1)

            read_features("agg", None)
            root(rstd[:, :], rstd[:, :])
            act.wait_ge(nmr_ready, 1)
            for t in range(NT):
                a_(x0[:, t, :], x1[:, t, :], ACT.Identity, scale=rstd[:, t:t + 1], bias=nmr[:, t:t + 1]).then_inc(x0_ready, 1)
            root(rstd[:, :], rstd[:, :])
            act.wait_ge(cols_in, 16 * 6)
            act.wait_ge(r_hid, 1)
            a_(hid[:, :], PS[:, O_BANK:O_BANK + 1], ACT.Gelu, bias=rb1[:, :]).then_inc(r_gelu, 1)
            act.wait_ge(r_max, 1)
            a_(rt[0:1, 1, :], rt[0:1, 0, :], ACT.Exp, bias=rt[0:1, 2, 0:1], accum_out=rt[0:1, 2, 1:2]).then_inc(r_exp, 1)

            def scaled_features(base, *norm):
                for m in range(KD):
                    b = m % 2
                    act.wait_ge(zT_done, base + m + 1)
                    if m >= 2:
                        act.wait_ge(zT_dve, base + m - 1)
                    for dst, (weight, bias) in zip((y32[b], xt32[m]), norm):
                        src = PS[:, b * ACC:b * ACC + 1024].rearrange("p (c n) -> p c n", n=512)[:, :, 0:500]
                        affine = dict(scale=norms[:, weight, m:m + 1], bias=norms[:, bias, m:m + 1])
                        a_(dst[:, 0:1000].rearrange("p (c n) -> p c n", n=500), src, ACT.Identity, **affine)
                        last = a_(dst[:, 1000:1250], PS[:, b * ACC + 1024:b * ACC + 1024 + 250], ACT.Identity, **affine)
                    last.then_inc(zT_act, 1)

            act.wait_ge(cols_in, 16 * 6)
            act.wait_ge(y_split, FBASE["agg"] + 4 + 2)
            scaled_features(0, (0, 1), (2, 3))
            act.wait_ge(qb_ready, 1)
            act.wait_ge(zT_dve, 4)
            read_features("SPK", sp_b[:, 0, :])
            read_features("SPQ", q_b[:, 0, :], scale=0.125 / WS)

            def attention(a):
                S = att[a]

                def exps(T, h, it):
                    if T >= NT:
                        return
                    act.wait_ge(S["max_done"], T * H + h + 1 + it * PER2["step"])
                    done = t_before(a, *((T, h - 1) if h else (T - 1, H - 1)), 0) if (T or h) else 0
                    if T * H + h >= 2:
                        act.wait_ge(S["t_full"], done + it * PER2["turn"])
                        c2 = c_before(a, *((T, h - 1) if h else (T - 1, H - 1)), 2)
                        if c2 > 0:
                            act.wait_ge(S["t2_full"], c2 + it * PER2["step"])
                    n_ = TP * key_tiles(a, T)
                    a_(prob[h % 2][:, 0:n_], PS[0:TP, (h % 2) * ACC:(h % 2) * ACC + n_], ACT.Exp, bias=nmax[:, h % 2:h % 2 + 1],
                       accum_out=rsum[:, T % 2, h:h + 1]).then_inc(S["exp_done"], 1)

                def output(T, it):
                    turn = t_before(a, T, 3, 0) if T < NT else t_before(a, NT - 1, H - 1, len(chunks(a, NT - 1))) + 1
                    act.wait_ge(S["t_full"], turn + it * PER2["turn"])
                    if T > 1:
                        act.wait_ge(S["oT_lo"], T - 1 + it * PER2["tile"])
                    a_(oT, PS[:, T_BANK:T_BANK + KD * TP].rearrange("p (k n) -> p k n", n=TP), ACT.Copy).then_inc(S["t_free"], 1)
                    act.wait_ge(S["t_free"], turn + it * PER2["turn"])
                    a_(at_[0][:, :, tile_columns(T - 1, it)], oT, ACT.Copy).then_inc(S["oT_hi"], 1)

                def high(T, h, it, c):
                    c0, c1 = chunks(a, T)[c]
                    act.wait_ge(S["t_free"], t_before(a, T, h, c + 1) + it * PER2["turn"])
                    if T * H + h >= 2:
                        act.wait_ge(S["av_done"], T * H + h - 1 + it * PER2["step"])
                    a_(pT_hi[h % 2][:, c0:c1, :], transposed_group(a, T, h, c), ACT.Copy).then_inc(S[f"hi_{c}"], 1)

                def body(T, it):
                    for h in range(H):
                        exps(*((T, h + 1) if h + 1 < H else (T + 1, 0)), it)
                        high(T, h, it, 0)
                        if len(chunks(a, T)) > 1:
                            act.wait_ge(S["t_full"], t_before(a, T, h, 2) + it * PER2["turn"])
                            wait_split(act, a, "lo", T, h, 1, it, 0)
                            c0, c1 = chunks(a, T)[1]
                            a_(transposed_group(a, T, h, 1),
                               PS[0:TP, T_BANK:T_BANK + (c1 - c0) * TP].rearrange("p (k n) -> p k n", n=TP),
                               ACT.Copy).then_inc(S["t_free"], 1)
                            high(T, h, it, 1)
                        if h == 2 and T >= 1:
                            output(T, it)

                exps(0, 0, 0)
                attention_tiles(act, a, body)
                output(NT, 0)

            attention(0)
            read_features("SPO", sp_ob)
            act.wait_ge(tmb_in, 16)
            read_features("TMK", tm_b[:, 0, :])
            read_features("TMQ", q_b[:, 1, :], scale=0.125 / WS)
            attention(1)
            read_features("TMP", tm_b[:, 2, :])
            read_features("CRQ", q_b[:, 2, :], scale=0.125 / WS)
            read_features("CRK", cr_b[:, 1, :])
            attention(2)
            root(rstd[:, :], rstd[:, :])
            act.wait_ge(nmr_ready, 2)
            for t in range(Z2_DVE, NT):
                last = a_(z2[:, t, :], x2[:, t, :], ACT.Identity, scale=rstd[:, t:t + 1], bias=nmr[:, t:t + 1])
            last.then_inc(z2_act, 1)
            scaled_features(4, (4, 5))
            act.wait_ge(zT_dve, 8)
            for j in range(4):
                read_features(f"UP{j}", up_b[:, 4 * j:4 * j + 4], fn=ACT.Gelu)

        @block.vector
        def _(dve):
            v = nc.vector
            ds = bass.ds
            n = [0]

            def link(ins):
                n[0] += 1
                ins.then_inc(dve_ch, 1)
                dve.wait_ge(dve_ch, n[0])

            dve.wait_ge(edges_in, 64)
            dve.wait_ge(consts, 1)
            v.tensor_reduce(dmm[:, 0:1], dst_g, AX.X, ALU.min)
            link(v.tensor_reduce(dmm[:, 1:2], dst_g, AX.X, ALU.max))
            link(v.tensor_scalar(dmm[:, 0:1], dmm[:, 0:1], float(1 - WIN), None, ALU.add))
            link(v.tensor_scalar(win_t, win25, dmm[:, 0:1], None, ALU.is_ge))
            link(v.scalar_tensor_tensor(win_t, win25, dmm[:, 1:2], win_t, ALU.is_le, ALU.mult))
            v.tensor_scalar(win_v[:, 0:NW], win_t, group1[:, 0:1], None, ALU.mult)
            v.tensor_scalar(win_v[:, NW:2 * NW], win_t, groupr[:, 0:1], None, ALU.mult).then_inc(bounds_ready, 1)
            dve.wait_ge(conf_in, 16)
            link(v.tensor_scalar(ew, attr[:, 0, :], confw[:, 0:1], None, ALU.mult))
            link(v.scalar_tensor_tensor(ew, attr[:, 1, :], confw[:, 1:2], ew, ALU.mult, ALU.add))
            v.scalar_tensor_tensor(ew, attr[:, 2, :], confw[:, 2:3], ew, ALU.mult, ALU.add).then_inc(logit_ready, 1)
            link(v.tensor_copy(src_f, src_i))
            link(v.tensor_scalar(src_hi, src_f, float(TP), None, ALU.is_ge))
            for t in range(2, NT):
                link(v.scalar_tensor_tensor(src_hi, src_f, float(TP * t), src_hi, ALU.is_ge, ALU.add))
            link(v.scalar_tensor_tensor(src_lo, src_hi, float(-TP), src_f, ALU.mult, ALU.add))
            v.scalar_tensor_tensor(krel[0], dst_i, float(NT), src_hi, ALU.mult, ALU.add).then_inc(krel_ready, 1)
            v.tensor_tensor(hi_hot, src_hi.unsqueeze(2).broadcast_to([TP, EC, NT]),
                            iota[:, 0:NT].unsqueeze(1).broadcast_to([TP, EC, NT]), ALU.is_equal).then_inc(hi_ready, 1)

            source_hots(v, 0)
            dve.wait_ge(boundsT, 1)
            v.tensor_reduce(rmax[:, :], PS[0:2 * NW, 0:NG], AX.X, ALU.max).then_inc(rmax_ready, 1)

            def window_table():
                dve.wait_ge(rows_done, 1)
                link(v.tensor_scalar(rows[0:1, 0, 0:NW], PS[0:1, 512 + NW:512 + 2 * NW], -1.0, float(NG), ALU.mult, ALU.add))
                link(v.tensor_scalar(rows[0:1, 0, 0:NW], rows[0:1, 0, 0:NW], float(NG - 1), None, ALU.min))
                link(v.scalar_tensor_tensor(rows[0:1, 1, 0:NW], rows[0:1, 0, 0:NW], 1.0, PS[0:1, 512:512 + NW], ALU.add, ALU.max))
                link(v.tensor_tensor(rows[0:1, 2, 0:NW], rows[0:1, 1, 0:NW], rows[0:1, 0, 0:NW], ALU.subtract))
                cur, step = 2, 1
                while step < NW:
                    other = {2: 3, 3: 1, 1: 3}[cur]
                    v.tensor_copy(rows[0:1, other, 0:step], rows[0:1, cur, 0:step])
                    link(v.tensor_tensor(rows[0:1, other, step:NW], rows[0:1, cur, step:NW], rows[0:1, cur, 0:NW - step], ALU.add))
                    cur, step = other, step * 2
                v.tensor_copy(visits[0:1, 0:1], rows[0:1, 0, 0:1])
                v.scalar_tensor_tensor(visits[0:1, 1:NW], rows[0:1, cur, 0:NW - 1], float(PACK), rows[0:1, 0, 1:NW], ALU.mult, ALU.add)
                v.tensor_scalar(visits[0:1, NW:NW + 1], rows[0:1, cur, NW - 1:NW], float(PACK), None, ALU.mult).then_inc(visits_ready, 1)

            def statistics(x, made=None):
                for t in range(NT):
                    if made is not None:
                        dve.wait_ge(made, t + 1)
                    last = v.bn_stats(stat[:, t, :], x[:, t, :])
                link(last)
                for t in range(NT):
                    last = v.bn_aggr(mv[:, t, :], stat[:, t, :])
                link(last)
                variances()

            def variances():
                link(v.tensor_scalar(var[:, :], mv[:, :, 1], EPS, None, ALU.add))
                v.tensor_copy(rstd[:, :], var[:, :]).then_inc(var_ready, 1)

            def means():
                v.scalar_tensor_tensor(nmr[:, :], mv[:, :, 0], -1.0, rstd[:, :], ALU.mult, ALU.mult).then_inc(nmr_ready, 1)

            def summed_up(name, dst, scale, x):
                for i in range(NT):
                    dve.wait_ge(accT_done, TBASE[name] + i + 1)
                    v.scalar_tensor_tensor(dst[:, i, :], PS[0:TP, (i % 2) * ACC:(i % 2) * ACC + D], scale(i), x[:, i, :],
                                           ALU.mult, ALU.add).then_inc(accT_free, 1)
                    dve.wait_ge(accT_free, TBASE[name] + i + 1 + 2)
                    link(v.bn_stats(stat[:, i, :], dst[:, i, :]))
                    last = v.bn_aggr(mv[:, i, :], stat[:, i, :])
                link(last)
                variances()

            def inverse_root(y, x):
                link(v.reciprocal(y, y))
                link(v.tensor_tensor(newton[:, :], y, y, ALU.mult))
                link(v.tensor_tensor(newton[:, :], newton[:, :], x, ALU.mult))
                link(v.tensor_scalar(newton[:, :], newton[:, :], -0.5, 1.5, ALU.mult, ALU.add))
                link(v.tensor_tensor(y, y, newton[:, :], ALU.mult))

            dve.wait_ge(x_in, 16)
            statistics(xs)
            def compared(part, subtracted):
                dve.wait_ge(lo_diff, subtracted * (EC // HOT_PARTS))
                v.tensor_scalar(lo_hot[:, part_chunks(part), :], lo_hot[:, part_chunks(part), :], 0.0, None,
                                ALU.is_equal).then_inc(lo_ready, 1)

            source_hots(v, 1)
            compared(3, 1)
            source_hots(v, 2)
            compared(4, 2)
            dve.wait_ge(ew_ready, 1)
            link(v.tensor_scalar(ew, ew, 0.0, ES, ALU.max, ALU.mult))
            link(v.tensor_copy(w16, ew))
            link(v.tensor_copy(w_hi, w16))
            link(v.tensor_tensor(w_lo, ew, w_hi, ALU.subtract))
            link(v.tensor_scalar(w_ratio, w_hi, 1e-30, None, ALU.max))
            link(v.reciprocal(w_ratio, w_ratio))
            link(v.scalar_tensor_tensor(w_ratio, w_ratio, LS, w_lo, ALU.mult, ALU.mult))
            window_table()
            dve.wait_ge(std_ready, 1)
            inverse_root(rstd[:, :], var[:, :])
            dve.wait_ge(deg_done, 1)
            v.tensor_copy(deg3, PS[0:3 * NT, 1024:1024 + 3 * TP]).then_inc(deg3_ready, 1)
            dve.wait_ge(deg_done, 2)
            at = [1536 + (3 * NT + NT) * c for c in range(3)]
            link(v.tensor_copy(deg[:, :], PS[0:TP, at[0]:at[0] + NT]))
            for c in (1, 2):
                link(v.tensor_tensor(deg[:, :], deg[:, :], PS[0:TP, at[c]:at[c] + NT], ALU.add))
            link(v.tensor_scalar(dis_s[:, :], deg[:, :], 0.0, None, ALU.is_gt))
            link(v.tensor_scalar(deg[:, :], deg[:, :], 1.0, None, ALU.max))
            v.tensor_copy(dis[:, :], deg[:, :]).then_inc(var_ready, 1)
            dve.wait_ge(std_ready, 2)
            inverse_root(dis[:, :], deg[:, :])
            link(v.tensor_tensor(dis[:, :], dis[:, :], dis_s[:, :], ALU.mult))
            link(v.scalar_tensor_tensor(rstd[:, :], rstd[:, :], WS, dis[:, :], ALU.mult, ALU.mult))
            v.tensor_scalar(dis_s[:, :], dis[:, :], 1.0 / WS, None, ALU.mult)
            v.scalar_tensor_tensor(nmr[:, :], mv[:, :, 0], -1.0, rstd[:, :], ALU.mult, ALU.mult).then_inc(xs_scale, 1)

            dve.wait_ge(visits_ready, 1)

            def key_hots(p, visit, group):
                for g in range(GC):
                    dve.wait_ge(hot_free[g], visit + 1)
                    c = ds(group * GC + g, 1)
                    v.tensor_scalar(key_hot[:, g, :], iota[:, :], krel[p][:, c], w_hi[:, c],
                                    ALU.is_equal, ALU.mult).then_inc(key_made[g], 1)

            windows(dve, key_hots, lambda w, p: dve.wait_ge(krel_ready, w + 1))

            dve.wait_ge(krel_ready, NW + 1)
            dve.wait_ge(win_free, NW + 2)
            a, b = (x[(NW - 1) % 2] for x in (high_part, low_part))
            link(v.tensor_tensor(a, a, b, ALU.add))
            whole = a.rearrange("p (a d) -> p a d", a=NT)
            link(v.tensor_copy(window_adj(NW - 1, 0), whole))
            v.tensor_tensor(window_adj(NW - 1, 1), whole, window_adj(NW - 1, 0), ALU.subtract).then_inc(last_added, 1)
            dve.wait_ge(xs_ready, 2 * NT)
            dve.wait_ge(win_done, NW)
            for t in range(NT):
                link(v.tensor_copy(xs_split[0][:, t, :], xs[:, t, :]))
                v.tensor_tensor(xs_split[1][:, t, :], xs[:, t, :], xs_split[0][:, t, :], ALU.subtract).then_inc(xs_halves, 1)
            dve.sem_inc(y_split, 2)
            dve.sem_inc(accT_free, 2)

            def split_features(name, dst, moved=None, moved_base=0, per=0, add=None, off=0):
                f = FBASE[name]
                with dve.Fori(0, 2) as mm:
                    for b in range(2):
                        m = mm * 2 + b
                        dve.wait_ge(accF_read, m + (f + 1 + 2))
                        if dst is None:
                            dve.wait_ge(moved[b], mm * per + (moved_base + per))
                            hi, lo = part_hi[b].unsqueeze(1), part_lo[b].unsqueeze(1)
                        else:
                            hi, lo = dst[0][:, ds(m + off, 1), :], dst[1][:, ds(m + off, 1), :]
                        y = y32[b].unsqueeze(1)
                        if add is not None:
                            for p in add:
                                v.tensor_tensor(y, y, p[:, ds(m, 1), :], ALU.add).then_inc(res_done, 1)
                                dve.wait_ge(res_done, m * 2 + (1 if p is add[0] else 2))
                        v.tensor_scalar(hi, y, 1.0, None, ALU.mult).then_inc(hi_done, 1)
                        dve.wait_ge(hi_done, m + (f + 1))
                        v.tensor_tensor(lo, y, hi, ALU.subtract).then_inc(y_split, 1)

            split_features("agg", agg)
            dve.wait_ge(xb_ready, 1)
            summed_up("LIN", x1, lambda i: dis_s[:, i:i + 1], xb)
            dve.sem_inc(x1_ready, 1)
            dve.wait_ge(std_ready, 3)
            inverse_root(rstd[:, :], var[:, :])
            means()
            statistics(x0, x0_ready)

            def normalised(dst, x, tiles):
                for t in tiles:
                    last = v.tensor_scalar(dst[:, t, :], x[:, t, :], mv[:, t, 0:1], rstd[:, t:t + 1], ALU.subtract, ALU.mult)
                return last

            dve.wait_ge(std_ready, 4)
            inverse_root(rstd[:, :], var[:, :])
            dve.wait_ge(r_pool, 1)
            v.tensor_scalar(means_row, PS[0:1, O_BANK:O_BANK + D], 1.0 / N, None, ALU.mult).then_inc(r_row, 1)
            dve.wait_ge(r_pool, 2)
            v.tensor_copy(pooled[:, :], PS[:, T_BANK:T_BANK + KD]).then_inc(r_poolc, 1)
            normalised(z0, x0, range(NT // 2))
            dve.wait_ge(cols_in, 16 * 6)
            dve.wait_ge(r_log, 1)
            link(v.tensor_tensor(rt[0:1, 0, :], PS[0:1, T_BANK:T_BANK + 8], rb2[:, :], ALU.add))
            v.tensor_reduce(rt[0:1, 2, 0:1], rt[0:1, 0, :], AX.X, ALU.max, negate=True).then_inc(r_max, 1)
            normalised(z0, x0, range(NT // 2, NT)).then_inc(z0_ready, 1)
            dve.wait_ge(r_exp, 1)
            link(v.reciprocal(rt[0:1, 2, 2:3], rt[0:1, 2, 1:2]))
            link(v.tensor_scalar(rt[0:1, 1, :], rt[0:1, 1, :], rt[0:1, 2, 2:3], None, ALU.mult))
            link(v.tensor_reduce(rt[0:1, 3, 0:2], rt[0:1, 1, :].rearrange("p (a b) -> p a b", a=2), AX.X, ALU.max))
            for a in range(2):
                link(v.scalar_tensor_tensor(rt[0:1, 4, 4 * a:4 * a + 4], rt[0:1, 1, 4 * a:4 * a + 4], rt[0:1, 3, a:a + 1],
                                            rt[0:1, 7, 4 * a:4 * a + 4], ALU.is_equal, ALU.mult))
            link(v.tensor_reduce(rt[0:1, 5, 0:2], rt[0:1, 4, :].rearrange("p (a b) -> p a b", a=2), AX.X, ALU.max))
            v.tensor_scalar(chosen[:, :], rt[0:1, 5, 0:2], -1.0, 4.0, ALU.mult, ALU.add).then_inc(r_idx, 1)

            for m in range(KD):
                b = m % 2
                dve.wait_ge(zT_act, m + 1)
                link(v.tensor_copy(xn[0][:, m, :], y32[b]))
                v.tensor_tensor(xn[1][:, m, :], y32[b], xn[0][:, m, :], ALU.subtract).then_inc(zT_dve, 1)
            for m in range(KD):
                v.tensor_copy(xt[0][:, m, :], xt32[m]).then_inc(xt_high, 1)
            dve.wait_ge(spb_in, 32)
            dve.wait_ge(tmb_in, 16)
            dve.wait_ge(cols_in, 16 * 6)
            v.tensor_scalar(q_b[:, 0, :], sp_b[:, 1, :], 0.125, None, ALU.mult)
            v.tensor_scalar(q_b[:, 1, :], tm_b[:, 1, :], 0.125, None, ALU.mult)
            v.tensor_scalar(q_b[:, 2, :], cr_b[:, 0, :], 0.125, None, ALU.mult).then_inc(qb_ready, 1)

            def token_values(name, row_bias):
                dve.wait_ge(rows_in[name], 16)
                t0 = TBASE[name]
                n0 = ("SPV", "TMV", "CRV").index(name) * NT
                with dve.Fori(0, NT // 2) as ii:
                    for b in range(2):
                        i = ii * 2 + b
                        dve.wait_ge(accT_done, i + (t0 + 1))
                        v.scalar_tensor_tensor(otok[b], PS[0:TP, b * ACC:b * ACC + D], 1.0 / WS, row_bias[:, :],
                                               ALU.mult, ALU.add).then_inc(accT_free, 1)
                        y = otok[b].rearrange("p (h d) -> p h d", d=HD).unsqueeze(1)
                        dve.wait_ge(accT_free, i + (t0 + 1 + 2))
                        v.tensor_scalar(V[:, ds(i, 1), :, 0:HD], y, 1.0, None, ALU.mult).then_inc(v_hi, 1)
                        dve.wait_ge(v_hi, i + (n0 + 1))
                        v.tensor_tensor(V[:, ds(i, 1), :, HD:2 * HD], y, V[:, ds(i, 1), :, 0:HD], ALU.subtract)

            def attention(a):
                S = att[a]

                def maxima(T, h, it):
                    if T >= NT:
                        return
                    dve.wait_ge(S["s_done"], T * H + h + 1 + it * PER2["step"])
                    n_ = TP * key_tiles(a, T)
                    v.tensor_reduce(nmax[:, h % 2:h % 2 + 1], PS[0:TP, (h % 2) * ACC:(h % 2) * ACC + n_], AX.X, ALU.max,
                                    negate=True).then_inc(S["max_done"], 1)

                def transposed(T, h, it, c):
                    if c >= len(chunks(a, T)):
                        return
                    c0, c1 = chunks(a, T)[c]
                    wait_split(dve, a, "lo", T, h, c, it, 0 if c else -1)
                    if c == 0:
                        dve.wait_ge(S["t_full"], t_before(a, T, h, 1) + it * PER2["turn"])
                    else:
                        dve.wait_ge(S["t2_full"], c_before(a, T, h, 2) + 1 + it * PER2["step"])
                    at = T_BANK if c == 0 else third_group(h)
                    v.tensor_copy(transposed_group(a, T, h, c), PS[0:TP, at:at + (c1 - c0) * TP].rearrange("p (k n) -> p k n", n=TP)
                                  ).then_inc(S["t_free" if c == 0 else "t2_free"], 1)

                def third_high(T, h, it):
                    if len(chunks(a, T)) < 3:
                        return
                    c0, c1 = chunks(a, T)[2]
                    dve.wait_ge(S["t2_free"], c_before(a, T, h, 2) + 1 + it * PER2["step"])
                    if T * H + h >= 2:
                        dve.wait_ge(S["av_done"], T * H + h - 1 + it * PER2["step"])
                    v.tensor_copy(pT_hi[h % 2][:, c0:c1, :], transposed_group(a, T, h, c)).then_inc(S["hi_2"], 1)

                o = PS[0:TP, O_BANK:O_BANK + D].rearrange("p (h d) -> p h d", d=2 * HD)

                def output_inverses(T, half, it):
                    heads, n_ = slice(4 * half, 4 * half + 4), 2 * T + half
                    dve.wait_ge(S["exp_done"], T * H + 4 * half + 4 + it * PER2["step"])
                    if n_:
                        dve.wait_ge(S["o_ready"], n_ + it * PER2["half"])
                    v.reciprocal(rinv[:, T % 2, heads], rsum[:, T % 2, heads]).then_inc(o_ch, 1)

                def output_hi(T, half, it):
                    dve.wait_ge(S["av_done"], T * H + 4 * half + 4 + it * PER2["step"])
                    v.tensor_copy(osum, o[:, :, 0:HD]).then_inc(o_ch, 1)

                def output_sum(T, half, it):
                    dve.wait_ge(o_ch, 2 * (2 * a * NT + 2 * T + half + 1) + it * (2 * PER2["half"]))
                    v.tensor_tensor(osum, o[:, :, HD:2 * HD], osum, ALU.add).then_inc(S["o_read"], 1)

                def output_scaled(T, half, it):
                    heads = slice(4 * half, 4 * half + 4)
                    dve.wait_ge(S["o_read"], 2 * T + half + 1 + it * PER2["half"])
                    v.tensor_tensor(otok[T % 2].rearrange("p (h d) -> p h d", d=HD)[:, heads, :], osum,
                                    rinv[:, T % 2, heads].unsqueeze(2).broadcast_to([TP, H // 2, HD]), ALU.mult).then_inc(S["o_ready"], 1)

                def body(T, it):
                    for h in range(H):
                        transposed(T, h, it, 0)
                        if h == 5 or (h == 1 and T >= 1):
                            output_scaled(*((T, 0) if h == 5 else (T - 1, 1)), it)
                        maxima(*((T, h + 2) if h + 2 < H else (T + 1, h + 2 - H)), it)
                        if h == 4 or (h == 0 and T >= 1):
                            output_inverses(*((T, 0) if h == 4 else (T - 1, 1)), it)
                        transposed(T, h, it, 2)
                        if h == 4 or (h == 0 and T >= 1):
                            output_hi(*((T, 0) if h == 4 else (T - 1, 1)), it)
                        third_high(T, h, it)
                        if h == 4 or (h == 0 and T >= 1):
                            output_sum(*((T, 0) if h == 4 else (T - 1, 1)), it)

                maxima(0, 0, 0)
                maxima(0, 1, 0)
                attention_tiles(dve, a, body)
                for part in (output_inverses, output_hi, output_sum, output_scaled):
                    part(NT - 1, 1, 0)

            split_features("SPK", None, k_moved, 0, 64)
            keys_moved(dve, 1)
            split_features("SPQ", None, q_moved, 0, 128)
            token_values("SPV", bb[1])
            attention(0)
            split_features("SPO", so)
            split_features("TMK", None, k_moved, 128, 64)
            keys_moved(dve, 2)
            split_features("TMQ", None, q_moved, 256, 128)
            token_values("TMV", bb[0])
            attention(1)
            split_features("TMP", to, add=to)
            split_features("CRQ", None, q_moved, 512, 128)
            queries_moved(dve, 3)
            split_features("CRK", None, k_moved, 256, 64)
            token_values("CRV", bb[1])
            attention(2)
            dve.wait_ge(x0b_ready, 1)
            summed_up("CRO", x2, lambda i: 1.0 / WS, x2)
            dve.wait_ge(std_ready, 5)
            inverse_root(rstd[:, :], var[:, :])
            means()
            normalised(z2, x2, range(Z2_DVE)).then_inc(z2_ready, 1)
            for m in range(KD):
                b = m % 2
                dve.wait_ge(zT_act, 4 + m + 1)
                link(v.tensor_copy(h2[0][:, m, :], y32[b]))
                v.tensor_tensor(h2[1][:, m, :], y32[b], h2[0][:, m, :], ALU.subtract).then_inc(zT_dve, 1)
            for j in range(4):
                split_features(f"UP{j}", gT, off=4 * j)
            dve.wait_ge(x1b_ready, 1)
            with dve.Fori(0, NT // 2) as ii:
                for b in range(2):
                    i = ii * 2 + b
                    dve.wait_ge(accT_done, i + (TBASE["DN"] + 1))
                    v.scalar_tensor_tensor(x2[:, ds(i, 1), :], PS[0:TP, b * ACC:b * ACC + D].unsqueeze(1), 1.0 / WS, x2[:, ds(i, 1), :],
                                           ALU.mult, ALU.add).then_inc(accT_free, 1)


def kernel(**inputs):
    import concourse.bacc as bacc
    from concourse.bass_utils import run_bass_kernel_spmd

    a = {k.replace("L0_", ""): np.asarray(v) for k, v in inputs.items()}

    def w(m):
        m = np.swapaxes(m, -1, -2)
        m = m.reshape(*m.shape[:-2], m.shape[-2] // 128, 128, m.shape[-1])
        return np.swapaxes(m, -3, -2)

    def cols(m):
        return np.swapaxes(m.reshape(*m.shape[:-1], m.shape[-1] // 128, 128), -1, -2)

    s_in, s_b = a["ffn_sp_in_w"].reshape(4, 3, D, D), a["ffn_sp_in_b"].reshape(4, 3, D)
    c_in, c_b = a["ffn_cross_in_w"].reshape(3, D, D), a["ffn_cross_in_b"].reshape(3, D)
    laid = {
        "x": a["x"],
        "src_t": a["src"].reshape(EC, TP).T, "dst_t": a["dst"].reshape(EC, TP).T,
        "dst_g": a["dst"].reshape(NG, GC * TP),
        "attr_t": a["edge_attr_3"].reshape(EC, TP, 3).transpose(1, 2, 0),
        "conf": np.concatenate([a["gnn_conf_w"], a["gnn_conf_b"][None]], axis=1),
        "lin_w": w(a["gnn_lin_w"]), "lin_b": a["gnn_lin_b"][None],
        "norms": np.stack([a[f"ffn_norm_{n}"] for n in ("s_w", "s_b", "t_w", "t_b", "mlp_w", "mlp_b")])
        .reshape(6, KD, 128).transpose(2, 0, 1),
        "r_w1": w(a["ffn_router_w1"]), "r_b1": a["ffn_router_b1"][:, None],
        "r_w2": a["ffn_router_w2"].T, "r_b2": a["ffn_router_b2"][None],
        "sp_w": w(s_in), "sp_kqb": cols(s_b[:, [1, 0]]).transpose(0, 2, 1, 3), "sp_vb": s_b[:, 2],
        "sp_ow": w(a["ffn_sp_out_w"]), "sp_ob": cols(a["ffn_sp_out_b"]),
        "tm_w": w(np.stack([a[f"ffn_t{n}_w"] for n in "qkvp"], axis=1)),
        "tm_kqpb": cols(np.stack([a[f"ffn_t{n}_b"] for n in "kqp"], axis=1)).transpose(0, 2, 1, 3), "tm_vb": a["ffn_tv_b"],
        "cr_w": w(c_in), "cr_qkb": cols(c_b[:2]).transpose(1, 0, 2), "cr_vb": c_b[2:],
        "cr_ow": w(a["ffn_cross_out_w"]), "cr_ob": a["ffn_cross_out_b"][None],
        "up_w": w(a["ffn_mlp_w1"].reshape(4, D, D)), "up_b": cols(a["ffn_mlp_b1"]),
        "dn_w": w(a["ffn_mlp_w2"].reshape(D, 4, D).transpose(1, 0, 2)), "dn_b": a["ffn_mlp_b2"][None],
    }
    nc = bacc.Bacc("TRN2", target_bir_lowering=False, num_devices=1, dynamic_dma_scratch_size=1024)
    arrays, handles = {}, {}
    for name, v in laid.items():
        v = np.ascontiguousarray(v)
        arrays[f"in_{name}"] = v
        handles[name] = nc.dram_tensor(f"in_{name}", v.shape, mybir.dt.from_np(v.dtype), kind="ExternalInput").ap()
    out = nc.dram_tensor("out", (N, D), F32, kind="ExternalOutput").ap()
    build(nc, handles, out)
    return run_bass_kernel_spmd(nc, [arrays], core_ids=[0]).results[0]["out"]
```
